# Optimizing a Trainium2 kernel written in Bass

```python
import numpy as np
import jax
import jax.numpy as jnp

def _softmax(x, axis=-1):
    return jax.nn.softmax(x, axis=axis)

def _gelu(x):
    return jax.nn.gelu(x, approximate=True)

def _silu(x):
    return jax.nn.silu(x)

def _sigmoid(x):
    return jax.nn.sigmoid(x)

def _layernorm(x, axis=-1, eps=1e-05):
    m = jnp.mean(x, axis=axis, keepdims=True)
    v = jnp.var(x, axis=axis, keepdims=True)
    return (x - m) / jnp.sqrt(v + eps)

def _scatter_add(tgt, idx, src, axis=0):
    return tgt.at[idx].add(src)

def _segment_sum(src, seg, n):
    return jax.ops.segment_sum(src, seg, n)
kernel_name = 'mk_dlrm_tower_d1_rec_r8_9b49f5'

def setup_inputs(seed: int=0):
    np.random.seed(seed)
    _w = jnp.asarray

    def _rec_inputs():
        import jax
        import jax.numpy as jnp
        _tk = jax.random.key(seed)
        dense_ctx = jax.random.normal(jax.random.fold_in(_tk, 190), (1024, 16), jnp.float32)
        ids = jnp.stack([jax.random.randint(jax.random.fold_in(_tk, 200 + f), (1024,), 0, v, jnp.int32) for f, v in enumerate([1250, 12500, 1250, 125000, 12500, 1000, 12500, 125000, 1250, 125000, 1000, 12500, 1000, 1250, 125000, 1250, 12500, 1000, 125000, 1250, 1000, 125000, 125000, 1000, 125000, 1000, 12500, 125000, 125000, 1000, 12500, 125000, 1000, 125000, 12500, 125000, 12500, 125000, 1000])], axis=1)
        tbl_0 = 0.05 * jax.random.normal(jax.random.fold_in(_tk, 500 + 0), (1250, 16), jnp.float32)
        tbl_1 = 0.05 * jax.random.normal(jax.random.fold_in(_tk, 500 + 1), (12500, 16), jnp.float32)
        tbl_2 = 0.05 * jax.random.normal(jax.random.fold_in(_tk, 500 + 2), (1250, 16), jnp.float32)
        tbl_3 = 0.05 * jax.random.normal(jax.random.fold_in(_tk, 500 + 3), (125000, 16), jnp.float32)
        tbl_4 = 0.05 * jax.random.normal(jax.random.fold_in(_tk, 500 + 4), (12500, 16), jnp.float32)
        tbl_5 = 0.05 * jax.random.normal(jax.random.fold_in(_tk, 500 + 5), (1000, 16), jnp.float32)
        tbl_6 = 0.05 * jax.random.normal(jax.random.fold_in(_tk, 500 + 6), (12500, 16), jnp.float32)
        tbl_7 = 0.05 * jax.random.normal(jax.random.fold_in(_tk, 500 + 7), (125000, 16), jnp.float32)
        tbl_8 = 0.05 * jax.random.normal(jax.random.fold_in(_tk, 500 + 8), (1250, 16), jnp.float32)
        tbl_9 = 0.05 * jax.random.normal(jax.random.fold_in(_tk, 500 + 9), (125000, 16), jnp.float32)
        tbl_10 = 0.05 * jax.random.normal(jax.random.fold_in(_tk, 500 + 10), (1000, 16), jnp.float32)
        tbl_11 = 0.05 * jax.random.normal(jax.random.fold_in(_tk, 500 + 11), (12500, 16), jnp.float32)
        tbl_12 = 0.05 * jax.random.normal(jax.random.fold_in(_tk, 500 + 12), (1000, 16), jnp.float32)
        tbl_13 = 0.05 * jax.random.normal(jax.random.fold_in(_tk, 500 + 13), (1250, 16), jnp.float32)
        tbl_14 = 0.05 * jax.random.normal(jax.random.fold_in(_tk, 500 + 14), (125000, 16), jnp.float32)
        tbl_15 = 0.05 * jax.random.normal(jax.random.fold_in(_tk, 500 + 15), (1250, 16), jnp.float32)
        tbl_16 = 0.05 * jax.random.normal(jax.random.fold_in(_tk, 500 + 16), (12500, 16), jnp.float32)
        tbl_17 = 0.05 * jax.random.normal(jax.random.fold_in(_tk, 500 + 17), (1000, 16), jnp.float32)
        tbl_18 = 0.05 * jax.random.normal(jax.random.fold_in(_tk, 500 + 18), (125000, 16), jnp.float32)
        tbl_19 = 0.05 * jax.random.normal(jax.random.fold_in(_tk, 500 + 19), (1250, 16), jnp.float32)
        tbl_20 = 0.05 * jax.random.normal(jax.random.fold_in(_tk, 500 + 20), (1000, 16), jnp.float32)
        tbl_21 = 0.05 * jax.random.normal(jax.random.fold_in(_tk, 500 + 21), (125000, 16), jnp.float32)
        tbl_22 = 0.05 * jax.random.normal(jax.random.fold_in(_tk, 500 + 22), (125000, 16), jnp.float32)
        tbl_23 = 0.05 * jax.random.normal(jax.random.fold_in(_tk, 500 + 23), (1000, 16), jnp.float32)
        tbl_24 = 0.05 * jax.random.normal(jax.random.fold_in(_tk, 500 + 24), (125000, 16), jnp.float32)
        tbl_25 = 0.05 * jax.random.normal(jax.random.fold_in(_tk, 500 + 25), (1000, 16), jnp.float32)
        tbl_26 = 0.05 * jax.random.normal(jax.random.fold_in(_tk, 500 + 26), (12500, 16), jnp.float32)
        tbl_27 = 0.05 * jax.random.normal(jax.random.fold_in(_tk, 500 + 27), (125000, 16), jnp.float32)
        tbl_28 = 0.05 * jax.random.normal(jax.random.fold_in(_tk, 500 + 28), (125000, 16), jnp.float32)
        tbl_29 = 0.05 * jax.random.normal(jax.random.fold_in(_tk, 500 + 29), (1000, 16), jnp.float32)
        tbl_30 = 0.05 * jax.random.normal(jax.random.fold_in(_tk, 500 + 30), (12500, 16), jnp.float32)
        tbl_31 = 0.05 * jax.random.normal(jax.random.fold_in(_tk, 500 + 31), (125000, 16), jnp.float32)
        tbl_32 = 0.05 * jax.random.normal(jax.random.fold_in(_tk, 500 + 32), (1000, 16), jnp.float32)
        tbl_33 = 0.05 * jax.random.normal(jax.random.fold_in(_tk, 500 + 33), (125000, 16), jnp.float32)
        tbl_34 = 0.05 * jax.random.normal(jax.random.fold_in(_tk, 500 + 34), (12500, 16), jnp.float32)
        tbl_35 = 0.05 * jax.random.normal(jax.random.fold_in(_tk, 500 + 35), (125000, 16), jnp.float32)
        tbl_36 = 0.05 * jax.random.normal(jax.random.fold_in(_tk, 500 + 36), (12500, 16), jnp.float32)
        tbl_37 = 0.05 * jax.random.normal(jax.random.fold_in(_tk, 500 + 37), (125000, 16), jnp.float32)
        tbl_38 = 0.05 * jax.random.normal(jax.random.fold_in(_tk, 500 + 38), (1000, 16), jnp.float32)
        _rk = jax.random.fold_in(_tk, 7)
        W_top1 = 0.05 * jax.random.normal(jax.random.fold_in(_tk, 801), (400, 512), jnp.float32)
        W_top2 = 0.0441942 * jax.random.normal(jax.random.fold_in(_tk, 802), (512, 256), jnp.float32)
        W_top3 = 0.0625 * jax.random.normal(jax.random.fold_in(_tk, 803), (256, 1), jnp.float32)
        b_top1 = jnp.zeros((512,), jnp.float32)
        b_top2 = jnp.zeros((256,), jnp.float32)
        return (dense_ctx, ids, tbl_0, tbl_1, tbl_2, tbl_3, tbl_4, tbl_5, tbl_6, tbl_7, tbl_8, tbl_9, tbl_10, tbl_11, tbl_12, tbl_13, tbl_14, tbl_15, tbl_16, tbl_17, tbl_18, tbl_19, tbl_20, tbl_21, tbl_22, tbl_23, tbl_24, tbl_25, tbl_26, tbl_27, tbl_28, tbl_29, tbl_30, tbl_31, tbl_32, tbl_33, tbl_34, tbl_35, tbl_36, tbl_37, tbl_38, W_top1, b_top1, W_top2, b_top2, W_top3)
    dense_ctx, ids, tbl_0, tbl_1, tbl_2, tbl_3, tbl_4, tbl_5, tbl_6, tbl_7, tbl_8, tbl_9, tbl_10, tbl_11, tbl_12, tbl_13, tbl_14, tbl_15, tbl_16, tbl_17, tbl_18, tbl_19, tbl_20, tbl_21, tbl_22, tbl_23, tbl_24, tbl_25, tbl_26, tbl_27, tbl_28, tbl_29, tbl_30, tbl_31, tbl_32, tbl_33, tbl_34, tbl_35, tbl_36, tbl_37, tbl_38, W_top1, b_top1, W_top2, b_top2, W_top3 = _rec_inputs()

    def _L0_rec_setup():
        import jax, jax.numpy as jnp
        import numpy as np
        B, F0, D = (256, 39, 16)
        CROSS = [128, 128, 128]
        key = jax.random.key(seed)
        k0, k1, k2, k3 = jax.random.split(key, 4)
        inputs = jax.random.normal(k0, (B, F0, D), dtype=jnp.float32)
        f0 = jax.random.normal(k1, (F0 * F0, CROSS[0]), dtype=jnp.float32) * 0.05
        f1 = jax.random.normal(k2, (CROSS[0] * F0, CROSS[1]), dtype=jnp.float32) * 0.05
        f2 = jax.random.normal(k3, (CROSS[1] * F0, CROSS[2]), dtype=jnp.float32) * 0.05
        return {'inputs': inputs, 'f0': f0, 'f1': f1, 'f2': f2}
    _L0_rec_all = _L0_rec_setup()
    _L0_rec_in = {k: v for k, v in _L0_rec_all.items() if k in ('f0', 'f1', 'f2')}
    del _L0_rec_all
    return {'dense_ctx': dense_ctx, 'ids': ids, 'tbl_0': tbl_0, 'tbl_1': tbl_1, 'tbl_2': tbl_2, 'tbl_3': tbl_3, 'tbl_4': tbl_4, 'tbl_5': tbl_5, 'tbl_6': tbl_6, 'tbl_7': tbl_7, 'tbl_8': tbl_8, 'tbl_9': tbl_9, 'tbl_10': tbl_10, 'tbl_11': tbl_11, 'tbl_12': tbl_12, 'tbl_13': tbl_13, 'tbl_14': tbl_14, 'tbl_15': tbl_15, 'tbl_16': tbl_16, 'tbl_17': tbl_17, 'tbl_18': tbl_18, 'tbl_19': tbl_19, 'tbl_20': tbl_20, 'tbl_21': tbl_21, 'tbl_22': tbl_22, 'tbl_23': tbl_23, 'tbl_24': tbl_24, 'tbl_25': tbl_25, 'tbl_26': tbl_26, 'tbl_27': tbl_27, 'tbl_28': tbl_28, 'tbl_29': tbl_29, 'tbl_30': tbl_30, 'tbl_31': tbl_31, 'tbl_32': tbl_32, 'tbl_33': tbl_33, 'tbl_34': tbl_34, 'tbl_35': tbl_35, 'tbl_36': tbl_36, 'tbl_37': tbl_37, 'tbl_38': tbl_38, 'W_top1': W_top1, 'b_top1': b_top1, 'W_top2': W_top2, 'b_top2': b_top2, 'W_top3': W_top3, 'L0_rec_f0': _L0_rec_in['f0'], 'L0_rec_f1': _L0_rec_in['f1'], 'L0_rec_f2': _L0_rec_in['f2']}

def reference(dense_ctx, ids, tbl_0, tbl_1, tbl_2, tbl_3, tbl_4, tbl_5, tbl_6, tbl_7, tbl_8, tbl_9, tbl_10, tbl_11, tbl_12, tbl_13, tbl_14, tbl_15, tbl_16, tbl_17, tbl_18, tbl_19, tbl_20, tbl_21, tbl_22, tbl_23, tbl_24, tbl_25, tbl_26, tbl_27, tbl_28, tbl_29, tbl_30, tbl_31, tbl_32, tbl_33, tbl_34, tbl_35, tbl_36, tbl_37, tbl_38, W_top1, b_top1, W_top2, b_top2, W_top3, L0_rec_f0, L0_rec_f1, L0_rec_f2):
    import jax
    import jax.numpy as jnp

    def _L0_rec_ref(inputs, f0, f1, f2):
        import jax, jax.numpy as jnp
        import numpy as np
        B, F0, D = (256, 39, 16)
        CROSS = [128, 128, 128]
        filters = [f0, f1, f2]
        x0 = inputs
        xk = inputs
        outs = []
        for W in filters:
            b, f, d = x0.shape
            g = xk.shape[1]
            z = jnp.einsum('bfd,bgd->bfgd', x0, xk).reshape(b, f * g, d)
            cur = jnp.einsum('bpd,pm->bmd', z, W)
            outs.append(cur)
            xk = cur
        result = jnp.concatenate(outs, axis=1)
        return jnp.sum(result, axis=-1)
    e = jnp.stack([tbl_0[ids[:, 0]], tbl_1[ids[:, 1]], tbl_2[ids[:, 2]], tbl_3[ids[:, 3]], tbl_4[ids[:, 4]], tbl_5[ids[:, 5]], tbl_6[ids[:, 6]], tbl_7[ids[:, 7]], tbl_8[ids[:, 8]], tbl_9[ids[:, 9]], tbl_10[ids[:, 10]], tbl_11[ids[:, 11]], tbl_12[ids[:, 12]], tbl_13[ids[:, 13]], tbl_14[ids[:, 14]], tbl_15[ids[:, 15]], tbl_16[ids[:, 16]], tbl_17[ids[:, 17]], tbl_18[ids[:, 18]], tbl_19[ids[:, 19]], tbl_20[ids[:, 20]], tbl_21[ids[:, 21]], tbl_22[ids[:, 22]], tbl_23[ids[:, 23]], tbl_24[ids[:, 24]], tbl_25[ids[:, 25]], tbl_26[ids[:, 26]], tbl_27[ids[:, 27]], tbl_28[ids[:, 28]], tbl_29[ids[:, 29]], tbl_30[ids[:, 30]], tbl_31[ids[:, 31]], tbl_32[ids[:, 32]], tbl_33[ids[:, 33]], tbl_34[ids[:, 34]], tbl_35[ids[:, 35]], tbl_36[ids[:, 36]], tbl_37[ids[:, 37]], tbl_38[ids[:, 38]]], axis=1)
    z = _L0_rec_ref(e, L0_rec_f0, L0_rec_f1, L0_rec_f2)
    z = z.reshape(z.shape[0], -1)
    h = jnp.concatenate([z, dense_ctx], axis=1)
    h = jnp.maximum(h @ W_top1 + b_top1, 0.0)
    h = jnp.maximum(h @ W_top2 + b_top2, 0.0)
    y = h @ W_top3
    return y

_drawn_inputs = setup_inputs


def setup_inputs(seed=0):
    import zlib

    import numpy as np

    out = dict(_drawn_inputs(seed))
    spreads = {'b_top1': (0.0, 0.585), 'b_top2': (0.0, 0.1)}
    factors = {'tbl_0': 4.526,
     'tbl_1': 4.844,
     'tbl_2': 4.552,
     'tbl_3': 4.688,
     'tbl_4': 4.829,
     'tbl_5': 4.897,
     'tbl_6': 4.766,
     'tbl_7': 4.613,
     'tbl_8': 5.086,
     'tbl_9': 4.443,
     'tbl_10': 4.959,
     'tbl_11': 4.617,
     'tbl_12': 4.577,
     'tbl_13': 4.377,
     'tbl_14': 4.521,
     'tbl_15': 4.856,
     'tbl_16': 5.013,
     'tbl_17': 4.76,
     'tbl_18': 4.857,
     'tbl_19': 4.993,
     'tbl_20': 4.824,
     'tbl_21': 4.673,
     'tbl_22': 4.664,
     'tbl_23': 4.814,
     'tbl_24': 4.531,
     'tbl_25': 4.436,
     'tbl_26': 4.851,
     'tbl_27': 4.768,
     'tbl_28': 4.604,
     'tbl_29': 4.851,
     'tbl_30': 5.043,
     'tbl_31': 4.534,
     'tbl_32': 4.853,
     'tbl_33': 4.572,
     'tbl_34': 4.464,
     'tbl_35': 4.684,
     'tbl_36': 4.722,
     'tbl_37': 4.873,
     'tbl_38': 4.995,
     'L0_rec_f1': 5.242,
     'L0_rec_f2': 8.0}
    for name, (base, spread) in spreads.items():
        noise = np.random.default_rng([zlib.crc32(name.encode()), seed]).standard_normal(out[name].shape)
        drawn = base * np.exp(spread * noise) if base else spread * noise
        out[name] = jnp.asarray(drawn.astype(out[name].dtype))
    for name, factor in factors.items():
        out[name] = (out[name] * factor).astype(out[name].dtype)
    return out
```

```python
from contextlib import ExitStack

import concourse.bass as bass
from concourse import mybir

ALU = mybir.AluOpType
ACT = mybir.ActivationFunctionType
AX = mybir.AxisListType
F32 = mybir.dt.float32
F32R = mybir.dt.float32r
I32 = mybir.dt.int32

P = 128
F = 39
D = 16
M = 128
ROWS = 1024
TILES = ROWS // P
QB = 4
BR = P // QB
NB = BR * D
GR, FR = 32, P // 32
GI, FI = M // GR, (F + FR - 1) // FR
L1 = GI * FI
SH = 3
L0 = 7
XROWS = F + (F - 1) // 2
CH = 4
CR = P // D
HID1, HID2 = 512, 256
H1T, H2T = HID1 // P, HID2 // P

WHOLE = (20, 24, 28, 32, 35, 38)
SPLIT = [i for i in range(L1) if i not in WHOLE]
NS = len(SPLIT)
POOL = [i for s, i in enumerate(SPLIT) if s % 2 == 1 and i < 38][:16]
L0_AFTER = {4 + 2 * k: k for k in range(L0)}

ZR = 4
SR = 5
LAG = 2
X_DMAS = 6
GATHERS = {0: 16, 1: 16, 2: F - 32}

PE_MAP0, PE_CTR, PE_G = 1, 7, (22, 25, 28, 31)
PE_XD, PE_Z2, PE_H1, PE_H2, PE_Y = (33, 35), (1, 3, 4, 5, 6), 10, 14, 18
PE_PREP = (12, 14, 16, 18)
ACT_Z0, ACT_CUR, ACT_CT, ACT_XBD, ACT_CH, ACT_G = 1, 4, 13, 14, 27, (28, 31, 34, 37)
ACT_XD, ACT_Z2, ACT_H1, ACT_H2, ACT_Y = (38, 39), 13, 16, 20, 24
ACT_PREP = (18, 20, 22, 24)
DVE_Z0, DVE_CL = 22, 29


def sequence(with_next):
    out = []
    for i in range(L1):
        out.append((1, i))
        if with_next and i in L0_AFTER:
            out.append((0, L0_AFTER[i]))
    return out


SEQ, SEQ_LAST = sequence(True), sequence(False)
PER = len(SEQ)


def is_split(tile):
    return tile[0] == 1 and tile[1] not in WHOLE


def on_pool(tile):
    return tile[0] == 1 and tile[1] in POOL


def rows_of(tile):
    layer, i = tile
    if layer == 0:
        return SH * F if i < L0 - 1 else 2 * F
    return P if i % FI < FI - 1 else (F - (FI - 1) * FR) * GR


class Place:

    def __init__(self, t, q):
        self.t, self.q = t, q
        fixed = isinstance(t, int)
        self.first_tile = fixed and t == 0
        self.last_tile = fixed and t == TILES - 1
        self.has_prev = not (self.first_tile and q == 0)
        self.has_prev2 = not (self.first_tile and q < 2)
        self.has_next = not (self.last_tile and q == QB - 1)
        self.has_next2 = not (self.last_tile and q >= QB - 2)
        self.seq = SEQ if self.has_next else SEQ_LAST

    def n(self, per, plus=0):
        return self.t * (QB * per) + (self.q * per + plus)

    def tiles(self, per, plus=0):
        return self.t * per + plus

    def done(self, p):
        return self.n(PER, L0 + p + 1)


def run_blocks(eng, body):
    for q in range(QB):
        body(Place(0, q))
    with eng.Fori(1, TILES - 1) as t:
        for q in range(QB):
            body(Place(t, q))
    for q in range(QB):
        body(Place(TILES - 1, q))


def position(tile, seq=SEQ):
    return seq.index(tile)


def slot_before(place, index, ring):
    if index >= ring:
        return index - ring
    if place.has_prev:
        return max(x for x in range(PER) if x % ring == index % ring) - PER
    return max(x for x in range(L0) if x % ring == index % ring) - L0


def cin_tower(nc, a, out):
    with ExitStack() as ctx:
        def sb(name, shape, dt=F32):
            return ctx.enter_context(nc.sbuf_tensor(name, shape, dt))

        def ps(name, shape):
            return ctx.enter_context(nc.psum_tensor(name, shape, F32))

        def sem(name):
            return ctx.enter_context(nc.semaphore(name))

        w0 = sb("w0", [P, L0, M])
        w1_hi = sb("w1_hi", [P, NS, M], F32R)
        w1_lo = sb("w1_lo", [P, NS, M], F32R)
        w1_whole = sb("w1_whole", [P, len(WHOLE), M])
        w2 = sb("w2", [P, F, M])
        wt1 = sb("wt1", [P, 3, HID1])
        wt1_ctx = sb("wt1_ctx", [D, HID1])
        wt2 = sb("wt2", [P, H1T, HID2])
        wt3 = sb("wt3", [P, H2T])
        bt1 = sb("bt1", [P, H1T])
        bt2 = sb("bt2", [P, H2T])
        ident = sb("ident", [P, P])
        rep_r = sb("rep_r", [P, P], F32R)
        mask = sb("mask", [P, CR])
        ids = sb("ids", [P, F], I32)
        emb = sb("emb", [P, F * D])
        x_t = sb("x_t", [F, P, D])
        x_cols = sb("x_cols", [P, P // CR, F])
        x_rep = sb("x_rep", [P, 2, FI, NB])
        x_rot = sb("x_rot", [P, L0 + 1, NB])
        z = sb("z", [P, ZR, NB])
        z_hi = sb("z_hi", [P, SR, NB], F32R)
        z_lo = sb("z_lo", [P, SR, NB], F32R)
        m0_hi = sb("m0_hi", [P, NB], F32R)
        m0_lo = sb("m0_lo", [P, NB], F32R)
        m1 = sb("m1", [P, NB])
        m1_t = sb("m1_t", [P, CH, M])
        x_diag = sb("x_diag", [P, CH, F + 1, CR])
        g2 = sb("g2", [P, F, P])
        z0_tile = sb("z0_tile", [P, P])
        sums = sb("sums", [P, 3, P])
        ctx_t = sb("ctx_t", [D, P])
        y = sb("y", [1, P])
        w1_stage = x_rep[:, 1].rearrange("p f (g m) -> p (f g) m", m=M)
        w1_by_maps = x_rep[:, 1].rearrange("p f (g m) -> p (f g) m", m=M)\
            .rearrange("p (g f) m -> p g f m", f=FI)
        tail = rows_of((1, FI - 1))
        w0_stage = g2[:, 0:L0, :]
        rep = g2[:, L0]
        h1 = g2[:, 0:H1T]
        h2 = g2[:, H1T:H1T + H2T]

        mrep_ps = ps("mrep_ps", [P, 2, NB])
        m0_ps = ps("m0_ps", [P, NB])
        m1_ps = ps("m1_ps", [P, 2, NB])
        g_ps = ps("g_ps", [P, 512])
        t_ps = ps("t_ps", [P, 2, 512])

        x_dram = nc.dram_tensor("x_scratch", (TILES, XROWS, P * D), F32, kind="Internal").ap()

        s_const = sem("s_const")
        s_w1_in = sem("s_w1_in")
        s_pad = sem("s_pad")
        s_w1_hi = sem("s_w1_hi")
        s_w = sem("s_w")
        s_ones = sem("s_ones")
        s_ids = sem("s_ids")
        s_gather = sem("s_gather")
        s_prep = sem("s_prep")
        s_xt = sem("s_xt")
        s_xdram = sem("s_xdram")
        s_xrep = [sem("s_xrep0"), sem("s_xrep1")]
        s_xrot = sem("s_xrot")
        s_xd = sem("s_xd")
        s_xcols = sem("s_xcols")
        s_z = sem("s_z")
        s_hi = sem("s_hi")
        s_lo_v = sem("s_lo_v")
        s_lo_p = sem("s_lo_p")
        s_pe = sem("s_pe")
        s_m0_hi = sem("s_m0_hi")
        s_m0_lo = sem("s_m0_lo")
        s_z0 = sem("s_z0")
        s_z0_tile = sem("s_z0_tile")
        s_mrep = sem("s_mrep")
        s_m1 = sem("s_m1")
        s_m1_tr = sem("s_m1_tr")
        s_m1_t = sem("s_m1_t")
        s_diag = sem("s_diag")
        s_g = sem("s_g")
        s_g2 = sem("s_g2")
        s_z2 = sem("s_z2")
        s_z2_in = sem("s_z2_in")
        s_ctx = sem("s_ctx")
        s_h1_ps = sem("s_h1_ps")
        s_h1 = sem("s_h1")
        s_h2_ps = sem("s_h2_ps")
        s_h2 = sem("s_h2")
        s_y_ps = sem("s_y_ps")
        s_y = sem("s_y")
        s_out = sem("s_out")

        s_met_pe, s_met_pool, s_met_sp = sem("s_met_pe"), sem("s_met_pool"), sem("s_met_sp")

        CONSTS = [
            (w0[0:SH * F, 0:L0 - 1, :], a["w0_a"]), (w0[0:F, L0 - 1, :], a["w0_last_a"]),
            (w0[F:2 * F, L0 - 1, :], a["w0_diag"]),
            (w0_stage[0:SH * F, 0:L0 - 1, :], a["w0_b"]), (w0_stage[0:F, L0 - 1, :], a["w0_last_b"]),
            (ident[:], a["ident"]), (rep, a["rep"]), (mask[:], a["mask"]),
            (w2[:], a["w2"]),
            (wt1[:], a["wt1"]), (wt1_ctx[:], a["wt1_ctx"]), (wt2[:], a["wt2"]), (wt3[:], a["wt3"]),
            (bt1[:], a["bt1"]), (bt2[:], a["bt2"]),
        ]
        ALL_CONSTS = 16 * len(CONSTS)

        block = ctx.enter_context(nc.Block())

        @block.sync
        def _(sp):
            def settled():
                sp.sem_inc(s_met_sp, 1)

            def load_ids(t):
                sp.dma_start(ids[:], a["ids"][bass.ds(t, 1)].rearrange("a p f -> p (a f)"))\
                    .then_inc(s_ids, 16)

            def store_x(t):
                for lo, n in ((0, F), (F, XROWS - F)):
                    sp.dma_start(x_dram[bass.ds(t, 1), lo:lo + n].rearrange("a f c -> f (a c)"),
                                 x_t[0:n].rearrange("f b d -> f (b d)")).then_inc(s_xdram, 16)

            def x_at(t, q, row, pattern):
                return bass.AP(x_dram.tensor, t * (XROWS * P * D) + (row * P * D + q * NB),
                               [*pattern, [1, NB]])

            def load_rep(t, q):
                row = P * D
                for j in range(FR):
                    n = (F - j + FR - 1) // FR
                    sp.dma_start(x_rep[GR * j:GR * (j + 1), q % 2, 0:n, :],
                                 x_at(t, q, j, [[0, GR], [FR * row, n]])).then_inc(s_xrep[q % 2], 16)

            def load_rot(t, q):
                row = P * D
                for s in range(SH):
                    n = L0 if s == 0 else L0 - 1
                    sp.dma_start(x_rot[F * s:F * (s + 1), 0:n, :],
                                 x_at(t, q, 1 + s, [[row, F], [SH * row, n]])).then_inc(s_xrot, 16)
                sp.dma_start(x_rot[F:2 * F, L0 - 1:L0 + 1, :],
                             x_at(t, q, 0, [[row, F], [0, 2]])).then_inc(s_xrot, 16)
                for s in (0, 2):
                    sp.dma_start(x_rot[F * s:F * (s + 1), L0, :],
                                 x_at(t, q, 0, [[row, F]])).then_inc(s_xrot, 16)

            load_ids(0)
            sp.dma_start(w1_by_maps[:, :, 0:FI - 1], a["w1_main"]).then_inc(s_w1_in, 16)
            sp.dma_start(w1_by_maps[0:tail, :, FI - 1], a["w1_tail"]).then_inc(s_w1_in, 16)
            for dst, src in CONSTS:
                sp.dma_start(dst, src).then_inc(s_const, 16)
            sp.wait_ge(s_xt, 4)
            store_x(0)
            sp.wait_ge(s_xdram, 32)
            load_rot(0, 0)
            load_rep(0, 0)
            sp.wait_ge(s_z, L0)
            load_rot(0, 1)

            def body(b):
                if b.q == 0 and not b.last_tile:
                    sp.wait_ge(s_gather, b.tiles(16 * F, 16 * F))
                    settled()
                    load_ids(b.t + 1)
                if b.q == 0 and not b.first_tile:
                    sp.dma_start(ctx_t[:], a["ctx"][bass.ds(b.t - 1, 1)].rearrange("a d r -> d (a r)"))\
                        .then_inc(s_ctx, 16)
                if b.has_next:
                    if b.has_prev:
                        sp.wait_ge(s_z, b.done(position((1, L1 - 1)) - PER))
                    else:
                        sp.wait_ge(s_w1_hi, 1)
                        sp.wait_ge(s_w, 2)
                    settled()
                    load_rep(*((b.t, b.q + 1) if b.q < QB - 1 else (b.t + 1, 0)))
                if b.q == 2 and not b.last_tile:
                    sp.wait_ge(s_xt, b.tiles(4, 8))
                    settled()
                    store_x(b.t + 1)
                    sp.wait_ge(s_xdram, b.tiles(32, 64))
                    settled()
                if b.has_next2:
                    sp.wait_ge(s_z, b.done(position((0, L0 - 1))))
                    settled()
                    load_rot(*((b.t, b.q + 2) if b.q < QB - 2 else (b.t + 1, b.q + 2 - QB)))
                if b.q == 2 and not b.first_tile:
                    sp.wait_ge(s_y, b.tiles(1))
                    settled()
                    sp.dma_start(out[bass.ds(b.t - 1, 1)], y[:])\
                        .then_inc(s_out, 16)
                if b.q == QB - 1 and not b.first_tile:
                    sp.wait_ge(s_out, b.tiles(16))
                    settled()

            run_blocks(sp, body)
            sp.dma_start(ctx_t[:], a["ctx"][TILES - 1]).then_inc(s_ctx, 16)
            sp.wait_ge(s_y, TILES)
            sp.dma_start(out[TILES - 1:TILES], y[:]).then_inc(s_out, 16)
            sp.wait_ge(s_out, 16 * TILES)

        @block.gpsimd
        def _(pool):
            def gather(f):
                nc.gpsimd.indirect_dma_start(
                    emb[:, D * f:D * (f + 1)], None, a[f"tbl_{f}"],
                    bass.IndirectOffsetOnAxis(ap=ids[:, f:f + 1], axis=0)).then_inc(s_gather, 16)

            pool.wait_ge(s_ids, 16)
            for f in range(F):
                gather(f)

            def body(b):
                todo = GATHERS.get(b.q, 0) if not b.last_tile else 0
                f = sum(GATHERS.get(x, 0) for x in range(b.q))
                if todo and b.q == 0:
                    pool.wait_ge(s_prep, b.tiles(4, 4))
                    pool.wait_ge(s_ids, b.tiles(16, 32))
                    pool.sem_inc(s_met_pool, 1)
                order = [x for x in b.seq if is_split(x)]
                for s, tile in enumerate(order):
                    if todo and (b.q == 2 or s % 2 == 0):
                        gather(f)
                        f, todo = f + 1, todo - 1
                    if not on_pool(tile):
                        continue
                    n = rows_of(tile)
                    pool.wait_ge(s_hi, b.n(NS, s + 1))
                    nc.gpsimd.tensor_tensor(z_lo[0:n, s % SR], z[0:n, b.seq.index(tile) % ZR],
                                            z_hi[0:n, s % SR].bitcast(F32), ALU.subtract)\
                        .then_inc(s_lo_p, 1)
                assert todo == 0

            run_blocks(pool, body)

        @block.scalar
        def _(act):
            def copy(dst, src, **kw):
                return nc.scalar.activation(dst, src, ACT.Copy, **kw)

            def move_x(t_count, r):
                act.wait_ge(s_prep, t_count + r + 1)
                copy(x_t[:, :, 4 * r:4 * r + 4].rearrange("f b d -> f d b"),
                     t_ps[0:F, r % 2, :].rearrange("f (d b) -> f d b", d=4)).then_inc(s_xt, 1)

            def move_m0_hi(b_count, after, sums_done):
                act.wait_ge(s_pe, after)
                act.wait_ge(s_z0, sums_done)
                if b_count is not None:
                    act.wait_ge(s_mrep, b_count)
                copy(m0_hi[:], m0_ps[:]).then_inc(s_m0_hi, 1)

            def layer2_diag(q, c):
                copy(x_diag[:, :, 0:F, c], x_cols[:, CH * q:CH * (q + 1), :],
                     scale=mask[:, c:c + 1]).then_inc(s_diag, 1)

            def move_g(q, c, count):
                act.wait_ge(s_g, count)
                at = BR * q + CR * c
                copy(g2[:, :, at:at + CR], g_ps[:, 0:F * CR].rearrange("p (f r) -> p f r", r=CR))\
                    .then_inc(s_g2, 1)
                copy(sums[:, 1, at:at + CR], g_ps[:, F * CR:(F + 1) * CR]).then_inc(s_g2, 1)

            def tower_step(step, t_done):
                if step == "z2":
                    act.wait_ge(s_z2, t_done)
                    copy(sums[:, 2], t_ps[:, 1, 0:P]).then_inc(s_z2_in, 1)
                elif step == "h1":
                    act.wait_ge(s_h1_ps, t_done)
                    for m in range(H1T):
                        nc.scalar.activation(h1[:, m], t_ps[:, 1, P * m:P * (m + 1)], ACT.Relu,
                                             bias=bt1[:, m:m + 1]).then_inc(s_h1, 1)
                elif step == "h2":
                    act.wait_ge(s_h2_ps, t_done)
                    for m in range(H2T):
                        nc.scalar.activation(h2[:, m], t_ps[:, 1, P * m:P * (m + 1)], ACT.Relu,
                                             bias=bt2[:, m:m + 1]).then_inc(s_h2, 1)
                else:
                    act.wait_ge(s_y_ps, t_done)
                    copy(y[:], t_ps[0:1, 1, 0:P]).then_inc(s_y, 1)

            act.wait_ge(s_w1_in, 32)
            act.wait_ge(s_pad, 1)
            at = 0
            for lo, hi in runs(SPLIT):
                last = copy(w1_hi[:, at:at + hi - lo], w1_stage[:, lo:hi])
                at += hi - lo
            for s, i in enumerate(WHOLE):
                last = copy(w1_whole[0:rows_of((1, i)), s], w1_stage[0:rows_of((1, i)), i])
            act.wait_ge(s_const, ALL_CONSTS)
            last = copy(rep_r[:], rep)
            last.then_inc(s_w1_hi, 1)
            for r in range(4):
                move_x(0, r)
            move_m0_hi(None, L0, 1)

            def body(b):
                splits = [x for x in b.seq if is_split(x)]
                for tile in b.seq:
                    layer, i = tile
                    if layer == 1:
                        if i == ACT_CUR and b.has_prev:
                            act.wait_ge(s_pe, b.done(-1))
                            if b.has_prev2:
                                act.wait_ge(s_m1_tr, b.n(1, -1))
                            copy(m1[:], m1_ps[:, (b.q - 1) % 2]).then_inc(s_m1, 1)
                        if i == ACT_CT and b.has_prev:
                            act.wait_ge(s_m1_tr, b.n(1))
                            if b.has_prev2:
                                act.wait_ge(s_g, b.n(CH, -CH))
                            copy(m1_t[:], t_ps[:, 0, :].rearrange("p (c m) -> p c m", m=M))\
                                .then_inc(s_m1_t, 1)
                        if 0 <= i - ACT_XBD < CR and b.has_prev:
                            if i == ACT_XBD:
                                act.wait_ge(s_xcols, b.tiles(2, 0 if b.q == 0 else 2))
                            layer2_diag((b.q - 1) % QB, i - ACT_XBD)
                        if i == ACT_CH and b.has_next:
                            move_m0_hi(b.n(GI, GI), b.done(position((0, L0 - 1))), b.n(1, 2))
                        if i in ACT_G and b.has_prev:
                            c = ACT_G.index(i)
                            move_g((b.q - 1) % QB, c, b.n(CH, c + 1 - CH))
                        if b.q == 0 and i in ACT_XD:
                            h = ACT_XD.index(i)
                            act.wait_ge(s_xd, b.tiles(2, h + 1))
                            if not b.first_tile:
                                act.wait_ge(s_diag, b.n(CR))
                            copy(x_cols[:, 8 * h:8 * h + 8],
                                 t_ps[:, h, 0:8 * F].rearrange("p (c f) -> p c f", f=F))\
                                .then_inc(s_xcols, 1)
                        if b.q == 1 and not b.first_tile:
                            for at, step in ((ACT_Z2, "z2"), (ACT_H1, "h1"), (ACT_H2, "h2"), (ACT_Y, "y")):
                                if i == at:
                                    tower_step(step, b.tiles(1))
                        if b.q == 2 and not b.last_tile and i in ACT_PREP:
                            r = ACT_PREP.index(i)
                            if r == 0:
                                act.wait_ge(s_xdram, b.tiles(32, 32))
                                act.wait_ge(s_xd, b.tiles(2, 2))
                            move_x(b.tiles(4, 4), r)
                        if b.q == QB - 1 and i == ACT_Z0:
                            act.wait_ge(s_z0, b.n(1, 1))
                            if not b.first_tile:
                                act.wait_ge(s_h1_ps, b.tiles(1))
                            copy(sums[:, 0], z0_tile[:]).then_inc(s_z0_tile, 1)
                    if is_split(tile):
                        s, n = splits.index(tile), rows_of(tile)
                        act.wait_ge(s_z, b.done(b.seq.index(tile)))
                        if (free := split_slot_free(b, splits, s)) is not None:
                            act.wait_ge(s_pe, free)
                        copy(z_hi[0:n, s % SR], z[0:n, b.seq.index(tile) % ZR]).then_inc(s_hi, 1)

            run_blocks(act, body)

            e = Place(TILES, 0)
            act.wait_ge(s_pe, e.done(-1) - L0)
            act.wait_ge(s_m1_tr, e.n(1, -1))
            copy(m1[:], m1_ps[:, (QB - 1) % 2]).then_inc(s_m1, 1)
            act.wait_ge(s_g, e.n(CH, -CH))
            for c in range(CR):
                layer2_diag(QB - 1, c)
            act.wait_ge(s_m1_tr, e.n(1))
            copy(m1_t[:], t_ps[:, 0, :].rearrange("p (c m) -> p c m", m=M)).then_inc(s_m1_t, 1)
            for c in range(CH):
                move_g(QB - 1, c, e.n(CH, c + 1 - CH))
            for step in ("z2", "h1", "h2", "y"):
                tower_step(step, TILES)

        @block.vector
        def _(dve):
            def zero_layer_products(slot, k):
                n = rows_of((0, k))
                return nc.vector.tensor_tensor(z[0:n, slot], x_rot[0:n, k], x_rot[0:n, L0], ALU.mult)

            def layer0_sums(q):
                nc.vector.tensor_reduce(z0_tile[:, BR * q:BR * (q + 1)],
                                        m0_ps[:].rearrange("p (b d) -> p b d", d=D), AX.X, ALU.add)\
                    .then_inc(s_z0, 1)

            def split_m0(blocks):
                dve.wait_ge(s_m0_hi, blocks)
                nc.vector.tensor_tensor(m0_lo[:], m0_ps[:], m0_hi[:].bitcast(F32), ALU.subtract)\
                    .then_inc(s_m0_lo, 1)

            nc.vector.memset(w1_by_maps[tail:P, :, FI - 1], 0.0).then_inc(s_pad, 1)
            dve.wait_ge(s_const, ALL_CONSTS)
            nc.vector.tensor_tensor(w0[0:SH * F, 0:L0 - 1], w0[0:SH * F, 0:L0 - 1],
                                    w0_stage[0:SH * F, 0:L0 - 1], ALU.add)
            nc.vector.tensor_tensor(w0[0:F, L0 - 1], w0[0:F, L0 - 1], w0_stage[0:F, L0 - 1], ALU.add)
            for c in range(CH):
                last = nc.vector.tensor_copy(x_diag[:, c, F], mask[:])
            last.then_inc(s_w, 1)
            dve.wait_ge(s_w1_hi, 1)
            at = 0
            for lo, hi in runs(SPLIT):
                n = hi - lo
                last = nc.vector.tensor_tensor(w1_lo[:, at:at + n], w1_stage[:, lo:hi],
                                               w1_hi[:, at:at + n].bitcast(F32), ALU.subtract)
                at += n
            last.then_inc(s_w, 1)

            dve.wait_ge(s_xrot, 16 * X_DMAS)
            for k in range(L0):
                if k >= ZR:
                    dve.wait_ge(s_pe, k - ZR + 1)
                zero_layer_products(k % ZR, k).then_inc(s_z, 1)
            dve.wait_ge(s_pe, L0)
            layer0_sums(0)
            split_m0(1)

            def split_z(b, seq, p, shift):
                tile = seq[p]
                if not is_split(tile) or on_pool(tile):
                    return
                s, n = [x for x in seq if is_split(x)].index(tile), rows_of(tile)
                dve.wait_ge(s_hi, b.n(NS, s + 1 - NS * shift))
                nc.vector.tensor_tensor(z_lo[0:n, s % SR], z[0:n, p % ZR],
                                        z_hi[0:n, s % SR].bitcast(F32), ALU.subtract)\
                    .then_inc(s_lo_v, 1)

            def body(b):
                for p, tile in enumerate(b.seq):
                    layer, i = tile
                    if layer == 1:
                        if i % FI == 0:
                            dve.wait_ge(s_mrep, b.n(GI, i // FI + 1))
                        if i == 0:
                            dve.wait_ge(s_xrep[b.q % 2], b.tiles(16 * FR * 2, 16 * FR * (b.q // 2 + 1)))
                        if i == DVE_Z0 and b.has_next:
                            dve.wait_ge(s_pe, b.done(position((0, L0 - 1))))
                            if b.q == QB - 1:
                                dve.wait_ge(s_z0_tile, b.tiles(1, 1))
                            layer0_sums((b.q + 1) % QB)
                        if i == DVE_CL and b.has_next:
                            split_m0(b.n(1, 2))
                    elif i == 0:
                        dve.wait_ge(s_xrot, b.n(16 * X_DMAS, 32 * X_DMAS))
                    wait_slot_free(dve, b, slot_before(b, p, ZR))
                    if layer == 0:
                        zero_layer_products(p % ZR, i).then_inc(s_z, 1)
                    else:
                        n, gi, fi = rows_of(tile), i // FI, i % FI
                        nc.vector.tensor_tensor(z[0:n, p % ZR], mrep_ps[0:n, gi % 2],
                                                x_rep[0:n, b.q % 2, fi], ALU.mult).then_inc(s_z, 1)
                    if p >= LAG:
                        split_z(b, b.seq, p - LAG, 0)
                    elif b.has_prev:
                        split_z(b, SEQ, PER + p - LAG, 1)

            def wait_slot_free(eng, b, before):
                seq, shift, p = (b.seq, 0, before) if before >= 0 else (SEQ, 1, before + PER)
                if before < 0 and not b.has_prev:
                    eng.wait_ge(s_pe, before + L0 + 1)
                    return
                tile = seq[p]
                if not is_split(tile):
                    eng.wait_ge(s_pe, b.done(before))
                elif on_pool(tile):
                    s = [x for x in seq if on_pool(x)].index(tile)
                    eng.wait_ge(s_lo_p, b.n(len(POOL), s + 1 - len(POOL) * shift))
                else:
                    mine = [x for x in seq if is_split(x) and not on_pool(x)]
                    eng.wait_ge(s_lo_v, b.n(len(mine), mine.index(tile) + 1 - len(mine) * shift))

            run_blocks(dve, body)
            e = Place(TILES, 0)
            for p in range(len(SEQ_LAST) - LAG, len(SEQ_LAST)):
                split_z(e, SEQ_LAST, p, 1)

        @block.tensor
        def _(pe):
            def prep(r):
                for d in range(4):
                    last = nc.tensor.transpose(
                        t_ps[0:F, r % 2, P * d:P * (d + 1)],
                        emb[:].rearrange("p (f d) -> p f d", d=D)[:, :, 4 * r + d], ident[:])
                last.then_inc(s_prep, 1)

            def layer0(slot, k, count):
                n = rows_of((0, k))
                pe.wait_ge(s_z, count)
                nc.tensor.matmul(m0_ps[:], w0[0:n, k], z[0:n, slot], start=(k == 0), stop=(k == L0 - 1))\
                    .then_inc(s_pe, 1)

            def repeat_maps(gi, blocks, free):
                pe.wait_ge(s_m0_hi, blocks)
                pe.wait_ge(s_m0_lo, blocks)
                if free is not None:
                    pe.wait_ge(s_z, free)
                rows = slice(GR * gi, GR * (gi + 1))
                nc.tensor.matmul(mrep_ps[:, gi % 2], rep_r[rows], m0_hi[rows], start=True, stop=False)
                nc.tensor.matmul(mrep_ps[:, gi % 2], rep_r[rows], m0_lo[rows], start=False, stop=True)\
                    .then_inc(s_mrep, 1)

            def turn_m1(blocks):
                pe.wait_ge(s_m1, blocks)
                for c in range(CH):
                    last = nc.tensor.transpose(t_ps[:, 0, M * c:M * (c + 1)],
                                               m1[:, P * c:P * (c + 1)], ident[:])
                last.then_inc(s_m1_tr, 1)

            def g_chunk(c, chunks, blocks, diags):
                pe.wait_ge(s_m1_t, blocks)
                pe.wait_ge(s_diag, diags)
                if c == 0:
                    pe.wait_ge(s_w, 1)
                if chunks is not None:
                    pe.wait_ge(s_g2, chunks)
                nc.tensor.matmul(g_ps[:, 0:(F + 1) * CR], m1_t[:, c],
                                 x_diag[:, c].rearrange("p f r -> p (f r)"), start=True, stop=True)\
                    .then_inc(s_g, 1)

            def layer2(part, parts, blocks):
                if part == 0:
                    pe.wait_ge(s_g2, blocks)
                per = (F + parts - 1) // parts
                for f in range(per * part, min(F, per * (part + 1))):
                    last = nc.tensor.matmul(t_ps[:, 1, 0:P], w2[:, f], g2[:, f],
                                            start=(f == 0), stop=(f == F - 1))
                if part == parts - 1:
                    last.then_inc(s_z2, 1)

            def hidden1(t_done):
                pe.wait_ge(s_z2_in, t_done)
                pe.wait_ge(s_z0_tile, t_done)
                pe.wait_ge(s_ctx, t_done * 16)
                for m in range(H1T):
                    cols = slice(P * m, P * (m + 1))
                    for k in range(3):
                        nc.tensor.matmul(t_ps[:, 1, cols], wt1[:, k, cols], sums[:, k],
                                         start=(k == 0), stop=False)
                    last = nc.tensor.matmul(t_ps[:, 1, cols], wt1_ctx[:, cols], ctx_t[:],
                                            start=False, stop=True)
                last.then_inc(s_h1_ps, 1)

            def hidden2(t_done):
                pe.wait_ge(s_h1, t_done * H1T)
                for m in range(H2T):
                    cols = slice(P * m, P * (m + 1))
                    for k in range(H1T):
                        last = nc.tensor.matmul(t_ps[:, 1, cols], wt2[:, k, cols], h1[:, k],
                                                start=(k == 0), stop=(k == H1T - 1))
                last.then_inc(s_h2_ps, 1)

            def output(t_done):
                pe.wait_ge(s_h2, t_done * H2T)
                for k in range(H2T):
                    last = nc.tensor.matmul(t_ps[0:1, 1, 0:P], wt3[:, k:k + 1], h2[:, k],
                                            start=(k == 0), stop=(k == H2T - 1))
                last.then_inc(s_y_ps, 1)

            pe.wait_ge(s_const, ALL_CONSTS)
            pe.wait_ge(s_gather, 16 * F)
            for r in range(4):
                if r >= 2:
                    pe.wait_ge(s_xt, r - 1)
                prep(r)
            pe.wait_ge(s_w, 1)
            for k in range(L0):
                layer0(k % ZR, k, k + 1)
            pe.wait_ge(s_w1_hi, 1)
            repeat_maps(0, 1, None)
            pe.wait_ge(s_w, 2)

            def body(b):
                splits = [x for x in b.seq if is_split(x)]
                by_dve = [x for x in splits if not on_pool(x)]
                by_pool = [x for x in splits if on_pool(x)]
                for p, tile in enumerate(b.seq):
                    layer, i = tile
                    if layer == 0:
                        if i == 0:
                            pe.wait_ge(s_m0_lo, b.n(1, 1))
                            pe.wait_ge(s_z0, b.n(1, 1))
                        layer0(p % ZR, i, b.done(p))
                        continue
                    if i == PE_MAP0:
                        repeat_maps(1, b.n(1, 1),
                                    b.done(position((1, L1 - 1)) - PER) if b.has_prev else None)
                    for gi in (2, 3):
                        if i == FI * (gi - 1) + 1:
                            repeat_maps(gi, b.n(1, 1), b.done(b.seq.index((1, FI * (gi - 1) - 1))))
                    if i == FI * 3 + 1 and b.has_next:
                        repeat_maps(0, b.n(1, 2), b.done(b.seq.index((1, FI * 3 - 1))))
                    if i == PE_CTR and b.has_prev:
                        if b.has_prev2:
                            pe.wait_ge(s_m1_t, b.n(1, -1))
                        if b.q == 1:
                            pe.wait_ge(s_xcols, b.tiles(2, 2))
                        if b.q == 3 and not b.last_tile:
                            pe.wait_ge(s_xt, b.tiles(4, 8))
                        turn_m1(b.n(1))
                    if i in PE_G and b.has_prev:
                        c = PE_G.index(i)
                        chunks = b.n(2 * CH, 2 * c - 2 * CH)
                        if not b.has_prev2 and c == 0:
                            chunks = None
                        g_chunk(c, chunks, b.n(1), b.n(CR))
                    if b.q == 0 and i in PE_XD:
                        h = PE_XD.index(i)
                        pe.wait_ge(s_xt, b.tiles(4, 4))
                        if h == 0 and b.has_prev:
                            pe.wait_ge(s_m1_t, b.n(1))
                        pe.sem_inc(s_met_pe, 1)
                        for c in range(8):
                            rows = slice(CR * (8 * h + c), CR * (8 * h + c + 1))
                            last = nc.tensor.transpose(t_ps[:, h, F * c:F * (c + 1)],
                                                       x_t[:, rows].rearrange("f b d -> f (b d)"),
                                                       ident[0:F, 0:F])
                        last.then_inc(s_xd, 1)
                    if b.q == 1 and not b.first_tile:
                        if i in PE_Z2:
                            if i == PE_Z2[0]:
                                pe.wait_ge(s_xcols, b.tiles(2, 2))
                            layer2(PE_Z2.index(i), len(PE_Z2), b.tiles(2 * CH * QB))
                        if i == PE_H1:
                            hidden1(b.t)
                        if i == PE_H2:
                            hidden2(b.t)
                        if i == PE_Y:
                            output(b.t)
                    if b.q == 2 and not b.last_tile and i in PE_PREP:
                        r = PE_PREP.index(i)
                        if r == 0:
                            pe.wait_ge(s_gather, b.tiles(16 * F, 32 * F))
                            pe.wait_ge(s_m1_t, b.n(1))
                            if not b.first_tile:
                                pe.wait_ge(s_y, b.tiles(1))
                            else:
                                pe.wait_ge(s_xcols, 2)
                        if r >= 2:
                            pe.wait_ge(s_xt, b.tiles(4, 4 + r - 1))
                        if r != 1:
                            pe.sem_inc(s_met_pe, 1)
                        prep(r)
                    bank = m1_ps[:, b.q % 2]
                    first, last_tile = i == 0, i == L1 - 1
                    if first and b.has_prev2:
                        pe.wait_ge(s_m1, b.n(1, -1))
                    n = rows_of(tile)
                    if is_split(tile):
                        s = splits.index(tile)
                        ws = SPLIT.index(i)
                        pe.wait_ge(s_hi, b.n(NS, s + 1))
                        nc.tensor.matmul(bank, w1_hi[0:n, ws], z_hi[0:n, s % SR], start=first, stop=False)
                        nc.tensor.matmul(bank, w1_lo[0:n, ws], z_hi[0:n, s % SR], start=False, stop=False)
                        if on_pool(tile):
                            pe.wait_ge(s_lo_p, b.n(len(by_pool), by_pool.index(tile) + 1))
                        else:
                            pe.wait_ge(s_lo_v, b.n(len(by_dve), by_dve.index(tile) + 1))
                        nc.tensor.matmul(bank, w1_hi[0:n, ws], z_lo[0:n, s % SR], start=False,
                                         stop=last_tile).then_inc(s_pe, 1)
                    else:
                        pe.wait_ge(s_z, b.done(p))
                        nc.tensor.matmul(bank, w1_whole[0:n, WHOLE.index(i)], z[0:n, p % ZR],
                                         start=first, stop=last_tile).then_inc(s_pe, 1)

            run_blocks(pe, body)

            e = Place(TILES, 0)
            pe.wait_ge(s_m1_t, e.n(1, -1))
            turn_m1(e.n(1))
            for c in range(CH):
                g_chunk(c, e.n(2 * CH, 2 * c - 2 * CH), e.n(1), e.n(CR))
            pe.wait_ge(s_y, TILES - 1)
            layer2(0, 1, 2 * CH * QB * TILES)
            hidden1(TILES)
            hidden2(TILES)
            output(TILES)


def runs(tiles):
    out = []
    for i in tiles:
        if out and out[-1][1] == i:
            out[-1][1] = i + 1
        else:
            out.append([i, i + 1])
    return out


def split_slot_free(b, splits, s):
    if s >= SR:
        return b.done(b.seq.index(splits[s - SR]))
    if not b.has_prev:
        return None
    before = [x for x in SEQ if is_split(x)]
    old = max(x for x in range(NS) if x % SR == s % SR)
    return b.done(SEQ.index(before[old]) - PER)


def kernel(**inputs):
    import numpy as np
    import concourse.bacc as bacc
    from concourse.bass_utils import run_bass_kernel_spmd

    x = {k: np.asarray(v) for k, v in inputs.items()}
    f0 = x["L0_rec_f0"].reshape(F, F, M)
    f1 = x["L0_rec_f1"].reshape(F, GI, GR, M)
    field = np.arange(F)
    shift = 1 + np.arange(SH)[:, None] + SH * np.arange(L0 - 1)[None, :]
    first = np.broadcast_to(field[None, :, None], (SH, F, L0 - 1))
    second = (field[None, :, None] + shift[:, None, :]) % F
    last = (field + (F - 1) // 2) % F
    whole = FR * (FI - 1)
    p = np.arange(P)
    arrays = {
        "ids": x["ids"].reshape(TILES, P, F),
        "ctx": x["dense_ctx"].reshape(TILES, P, D).transpose(0, 2, 1),
        "w0_a": f0[first, second].reshape(SH * F, L0 - 1, M),
        "w0_b": f0[second, first].reshape(SH * F, L0 - 1, M),
        "w0_last_a": f0[field, last], "w0_last_b": f0[last, field], "w0_diag": f0[field, field],
        "w1_main": f1[:whole].reshape(FI - 1, FR, GI, GR, M).transpose(1, 3, 2, 0, 4)
        .reshape(P, GI, FI - 1, M),
        "w1_tail": f1[whole:].transpose(0, 2, 1, 3).reshape((F - whole) * GR, GI, M),
        "w2": x["L0_rec_f2"].reshape(F, M, M).transpose(1, 0, 2),
        "wt1": x["W_top1"][:3 * M].reshape(3, M, HID1).transpose(1, 0, 2),
        "wt1_ctx": x["W_top1"][3 * M:],
        "wt2": x["W_top2"].reshape(H1T, P, HID2).transpose(1, 0, 2),
        "wt3": x["W_top3"].reshape(H2T, P).T,
        "bt1": x["b_top1"].reshape(H1T, P).T,
        "bt2": x["b_top2"].reshape(H2T, P).T,
        "ident": np.eye(P, dtype=np.float32),
        "rep": (p[:, None] % GR == p[None, :] % GR).astype(np.float32),
        "mask": (p[:, None] // D == np.arange(CR)[None, :]).astype(np.float32),
        **{f"tbl_{f}": x[f"tbl_{f}"] for f in range(F)},
    }
    arrays = {k: np.ascontiguousarray(v) for k, v in arrays.items()}
    nc = bacc.Bacc("TRN2", target_bir_lowering=False, num_devices=1)
    args = {k: nc.dram_tensor(f"in_{k}", v.shape, mybir.dt.from_np(v.dtype), kind="ExternalInput").ap()
            for k, v in arrays.items()}
    out = nc.dram_tensor("out", (ROWS, 1), F32, kind="ExternalOutput").ap()
    cin_tower(nc, args, out.rearrange("(t r) o -> t (r o)", t=TILES))
    r = run_bass_kernel_spmd(nc, [{f"in_{k}": v for k, v in arrays.items()}], core_ids=[0])
    return r.results[0]["out"]
```

```python
from contextlib import ExitStack

import concourse.bass as bass
from concourse import mybir

ALU = mybir.AluOpType
ACT = mybir.ActivationFunctionType
AX = mybir.AxisListType
F32 = mybir.dt.float32
F32R = mybir.dt.float32r
I32 = mybir.dt.int32

P = 128
F = 39
D = 16
M = 128
ROWS = 1024
TILES = ROWS // P
QB = 4
BR = P // QB
NB = BR * D
GR, FR = 32, P // 32
GI, FI = M // GR, (F + FR - 1) // FR
L1 = GI * FI
SH = 3
L0 = 7
XROWS = F + (F - 1) // 2
CH = 4
CR = P // D
HID1, HID2 = 512, 256
H1T, H2T = HID1 // P, HID2 // P

WHOLE = (20, 24, 28, 32, 35, 38)
SPLIT = [i for i in range(L1) if i not in WHOLE]
NS = len(SPLIT)
ON_POOL = (22, 8, 22, 24)
L0_AFTER = {6 + 2 * k: k for k in range(L0)}

ZR = 6
SR = 9
LAG = 2
XG = 2
X_DMAS = 6
GATHERS = {0: (8, 10, 3), 1: (F - 8, 0, 1)}

PE_MAP0, PE_M1, PE_G = 1, 9, (22, 24, 30, 32)
PE_PREP = (15, 17, 19, 21)
PE_XD = (20, 33)
PE_Z2, PE_H1, PE_H2, PE_Y = tuple(range(1, 11)), (17, 18, 19, 20), (30, 33), 39
ACT_Z0, ACT_M1, ACT_M1T, ACT_DIAG, ACT_M0, ACT_G = 1, 6, 13, 14, 26, (28, 29, 36, 37)
ACT_PREP, ACT_XD, ACT_Z2, ACT_H1, ACT_H2 = (18, 20, 22, 24), (26, 38), 14, 24, 36
ACT_Y = 3
DVE_Z0, DVE_M0 = 23, 28


def sequence(with_next):
    out = []
    for i in range(L1):
        out.append((1, i))
        if with_next and i in L0_AFTER:
            out.append((0, L0_AFTER[i]))
    return out


SEQ, SEQ_LAST = sequence(True), sequence(False)
PER = len(SEQ)


def is_split(tile):
    return tile[0] == 1 and tile[1] not in WHOLE


def on_pool(tile, q):
    if not is_split(tile):
        return False
    s = SPLIT.index(tile[1])
    return (s + 1) * ON_POOL[q] // NS > s * ON_POOL[q] // NS


def rows_of(tile):
    layer, i = tile
    if layer == 0:
        return SH * F if i < L0 - 1 else 2 * F
    return P if i % FI < FI - 1 else (F - (FI - 1) * FR) * GR


class Place:

    def __init__(self, t, q):
        self.t, self.q = t, q
        fixed = isinstance(t, int)
        self.first_tile = fixed and t == 0
        self.last_tile = fixed and t == TILES - 1
        self.has_prev = not (self.first_tile and q == 0)
        self.has_prev2 = not (self.first_tile and q < 2)
        self.has_next = not (self.last_tile and q == QB - 1)
        self.has_next2 = not (self.last_tile and q >= QB - 2)
        self.seq = SEQ if self.has_next else SEQ_LAST

    def n(self, per, plus=0):
        return self.t * (QB * per) + (self.q * per + plus)

    def tiles(self, per, plus=0):
        return self.t * per + plus

    def made_lo(self, q, s):
        here = on_pool((1, SPLIT[s]), q)

        def made(x, n=NS):
            return sum(on_pool((1, i), x) == here for i in SPLIT[:n])

        before = sum(made(x) for x in range(QB))
        total = sum(made(x) for x in range(q)) + made(q, s + 1)
        return self.t * before + (total if q <= self.q else total - before)

    def done(self, p):
        return self.n(PER, L0 + p + 1)


def run_blocks(eng, body):
    for q in range(QB):
        body(Place(0, q))
    with eng.Fori(1, TILES - 1) as t:
        for q in range(QB):
            body(Place(t, q))
    for q in range(QB):
        body(Place(TILES - 1, q))


def position(tile, seq=SEQ):
    return seq.index(tile)


def slot_before(place, index, ring):
    if index >= ring:
        return index - ring
    if place.has_prev:
        return max(x for x in range(PER) if x % ring == index % ring) - PER
    return max(x for x in range(L0) if x % ring == index % ring) - L0


def cin_tower(nc, a, out):
    with ExitStack() as ctx:
        def sb(name, shape, dt=F32):
            return ctx.enter_context(nc.sbuf_tensor(name, shape, dt))

        def ps(name, shape):
            return ctx.enter_context(nc.psum_tensor(name, shape, F32))

        def sem(name):
            return ctx.enter_context(nc.semaphore(name))

        w0 = sb("w0", [P, L0, M])
        w1_hi = sb("w1_hi", [P, NS, M], F32R)
        w1_lo = sb("w1_lo", [P, NS, M], F32R)
        w1_whole = sb("w1_whole", [P, len(WHOLE), M])
        w2 = sb("w2", [P, F, M])
        wt1 = sb("wt1", [P, 3, HID1])
        wt2 = sb("wt2", [P, H1T, HID2])
        wt3 = sb("wt3", [P, H2T])
        bt1 = sb("bt1", [P, H1T])
        bt2 = sb("bt2", [P, H2T])
        ident = sb("ident", [P, P])
        rep_r = sb("rep_r", [P, P], F32R)
        mask = sb("mask", [P, CR])
        ids = sb("ids", [P, F], I32)
        emb = sb("emb", [P, F * D])
        x_t_store = sb("x_t_store", [P, P * D])
        x_t = x_t_store[0:F].rearrange("f (b d) -> f b d", d=D)
        wt1_ctx = x_t_store[64:64 + D, 0:HID1]
        ctx_t = x_t_store[64:64 + D, HID1:HID1 + P]
        x_cols = sb("x_cols", [P, P // CR, F])
        x_rep = sb("x_rep", [P, FI, NB])
        x_rot = sb("x_rot", [P, L0 + 1, NB])
        z = sb("z", [P, ZR, NB])
        z_hi = sb("z_hi", [P, SR, NB], F32R)
        z_lo = sb("z_lo", [P, SR, NB], F32R)
        m0_hi = sb("m0_hi", [P, NB], F32R)
        m0_lo = sb("m0_lo", [P, NB], F32R)
        m1 = sb("m1", [P, NB])
        m1_t = sb("m1_t", [P, CH, M])
        x_diag = sb("x_diag", [P, CH, F + 1, CR])
        g2 = sb("g2", [P, F, P])
        z0_tile = sb("z0_tile", [P, P])
        sums = sb("sums", [P, 3, P])
        h1 = sb("h1", [P, H1T, P])
        h2 = sb("h2", [P, H2T, P])
        y = sb("y", [1, P])
        w1_stage = x_rep[:].rearrange("p f (g m) -> p (f g) m", m=M)
        w1_by_maps = x_rep[:].rearrange("p f (g m) -> p (f g) m", m=M)\
            .rearrange("p (g f) m -> p g f m", f=FI)
        tail = rows_of((1, FI - 1))
        w0_stage = g2[:, 0:L0, :]
        rep = g2[:, L0]

        mrep_ps = ps("mrep_ps", [P, 2, NB])
        m0_ps = ps("m0_ps", [P, NB])
        m1_ps = ps("m1_ps", [P, 2, NB])
        g_ps = ps("g_ps", [P, 512])
        t_ps = ps("t_ps", [P, 2, 512])

        def g_bank(c):
            return g_ps if c % 2 == 0 else t_ps[:, 0]

        x_dram = nc.dram_tensor("x_scratch", (TILES, XROWS, P * D), F32, kind="Internal").ap()

        s_const = sem("s_const")
        s_w1_in = sem("s_w1_in")
        s_pad = sem("s_pad")
        s_w1_hi = sem("s_w1_hi")
        s_w = sem("s_w")
        s_ones = sem("s_ones")
        s_ids = sem("s_ids")
        s_gather = sem("s_gather")
        s_prep = sem("s_prep")
        s_xt = sem("s_xt")
        s_xdram = sem("s_xdram")
        s_xrep = [sem(f"s_xrep{g}") for g in range(FI // XG)]
        s_xrot = sem("s_xrot")
        s_xd = sem("s_xd")
        s_xcols = sem("s_xcols")
        s_z = sem("s_z")
        s_hi = sem("s_hi")
        s_lo_v = sem("s_lo_v")
        s_lo_p = sem("s_lo_p")
        s_pe = sem("s_pe")
        s_m0_hi = sem("s_m0_hi")
        s_m0_lo = sem("s_m0_lo")
        s_z0 = sem("s_z0")
        s_z0_tile = sem("s_z0_tile")
        s_mrep = sem("s_mrep")
        s_m1 = sem("s_m1")
        s_m1_tr = sem("s_m1_tr")
        s_m1_t = sem("s_m1_t")
        s_diag = sem("s_diag")
        s_g = sem("s_g")
        s_g2 = sem("s_g2")
        s_z2 = sem("s_z2")
        s_z2_in = sem("s_z2_in")
        s_ctx = sem("s_ctx")
        s_h1_ps = sem("s_h1_ps")
        s_h1 = sem("s_h1")
        s_h2_ps = sem("s_h2_ps")
        s_h2 = sem("s_h2")
        s_y_ps = sem("s_y_ps")
        s_y = sem("s_y")
        s_out = sem("s_out")

        s_met_pe, s_met_pool, s_met_sp = sem("s_met_pe"), sem("s_met_pool"), sem("s_met_sp")

        CONSTS = [
            (w0[0:SH * F, 0:L0 - 1, :], a["w0_a"]), (w0[0:F, L0 - 1, :], a["w0_last_a"]),
            (w0[F:2 * F, L0 - 1, :], a["w0_diag"]),
            (w0_stage[0:SH * F, 0:L0 - 1, :], a["w0_b"]), (w0_stage[0:F, L0 - 1, :], a["w0_last_b"]),
            (ident[:], a["ident"]), (rep, a["rep"]), (mask[:], a["mask"]),
            (w2[:], a["w2"]),
            (wt1[:], a["wt1"]), (wt1_ctx, a["wt1_ctx"]), (wt2[:], a["wt2"]), (wt3[:], a["wt3"]),
            (bt1[:], a["bt1"]), (bt2[:], a["bt2"]),
        ]
        ALL_CONSTS = 16 * len(CONSTS)

        block = ctx.enter_context(nc.Block())

        @block.sync
        def _(sp):
            def settled():
                sp.sem_inc(s_met_sp, 1)

            def load_ids(t):
                sp.dma_start(ids[:], a["ids"][bass.ds(t, 1)].rearrange("a p f -> p (a f)"))\
                    .then_inc(s_ids, 16)

            def store_x(t):
                for lo, n in ((0, F), (F, XROWS - F)):
                    sp.dma_start(x_dram[bass.ds(t, 1), lo:lo + n].rearrange("a f c -> f (a c)"),
                                 x_t[0:n].rearrange("f b d -> f (b d)")).then_inc(s_xdram, 16)

            def x_at(t, q, row, pattern):
                return bass.AP(x_dram.tensor, t * (XROWS * P * D) + (row * P * D + q * NB),
                               [*pattern, [1, NB]])

            def load_rep(t, q, g):
                row = P * D
                for j in range(FR):
                    n = min(XG, (F - j + FR - 1) // FR - XG * g)
                    sp.dma_start(x_rep[GR * j:GR * (j + 1), XG * g:XG * g + n, :],
                                 x_at(t, q, FR * XG * g + j, [[0, GR], [FR * row, n]]))\
                        .then_inc(s_xrep[g], 16)

            def load_rot(t, q):
                row = P * D
                for s in range(SH):
                    n = L0 if s == 0 else L0 - 1
                    sp.dma_start(x_rot[F * s:F * (s + 1), 0:n, :],
                                 x_at(t, q, 1 + s, [[row, F], [SH * row, n]])).then_inc(s_xrot, 16)
                sp.dma_start(x_rot[F:2 * F, L0 - 1:L0 + 1, :],
                             x_at(t, q, 0, [[row, F], [0, 2]])).then_inc(s_xrot, 16)
                for s in (0, 2):
                    sp.dma_start(x_rot[F * s:F * (s + 1), L0, :],
                                 x_at(t, q, 0, [[row, F]])).then_inc(s_xrot, 16)

            load_ids(0)
            sp.dma_start(w1_by_maps[:, :, 0:FI - 1], a["w1_main"]).then_inc(s_w1_in, 16)
            sp.dma_start(w1_by_maps[0:tail, :, FI - 1], a["w1_tail"]).then_inc(s_w1_in, 16)
            for dst, src in CONSTS:
                sp.dma_start(dst, src).then_inc(s_const, 16)
            sp.wait_ge(s_xt, 4)
            store_x(0)
            sp.wait_ge(s_xdram, 32)
            load_rot(0, 0)
            sp.wait_ge(s_w1_hi, 1)
            sp.wait_ge(s_w, 2)
            for g in range(FI // XG):
                load_rep(0, 0, g)
            sp.wait_ge(s_z, L0)
            load_rot(0, 1)

            def body(b):
                if b.q == 0 and not b.last_tile:
                    sp.wait_ge(s_gather, b.tiles(16 * F, 16 * F))
                    settled()
                    load_ids(b.t + 1)
                if b.q == 0 and not b.first_tile:
                    sp.dma_start(ctx_t, a["ctx"][bass.ds(b.t - 1, 1)].rearrange("a d r -> d (a r)"))\
                        .then_inc(s_ctx, 16)
                if b.q == 2 and not b.last_tile:
                    sp.wait_ge(s_xt, b.tiles(4, 8))
                    settled()
                    store_x(b.t + 1)
                    sp.wait_ge(s_xdram, b.tiles(32, 64))
                    settled()
                if b.has_next2:
                    sp.wait_ge(s_z, b.done(position((0, L0 - 1))))
                    settled()
                    load_rot(*((b.t, b.q + 2) if b.q < QB - 2 else (b.t + 1, b.q + 2 - QB)))
                if b.has_next:
                    for g in range(FI // XG):
                        sp.wait_ge(s_z, b.done(position((1, L1 - FI + XG * (g + 1) - 1))))
                        settled()
                        load_rep(*((b.t, b.q + 1) if b.q < QB - 1 else (b.t + 1, 0)), g)
                if b.q == 2 and not b.first_tile:
                    sp.wait_ge(s_y, b.tiles(1))
                    settled()
                    sp.dma_start(out[bass.ds(b.t - 1, 1)], y[:])\
                        .then_inc(s_out, 16)
                if b.q == QB - 1 and not b.first_tile:
                    sp.wait_ge(s_out, b.tiles(16))
                    settled()

            run_blocks(sp, body)
            sp.dma_start(ctx_t, a["ctx"][TILES - 1]).then_inc(s_ctx, 16)
            sp.wait_ge(s_y, TILES)
            sp.dma_start(out[TILES - 1:TILES], y[:]).then_inc(s_out, 16)
            sp.wait_ge(s_out, 16 * TILES)

        @block.gpsimd
        def _(pool):
            def gather(f):
                nc.gpsimd.indirect_dma_start(
                    emb[:, D * f:D * (f + 1)], None, a[f"tbl_{f}"],
                    bass.IndirectOffsetOnAxis(ap=ids[:, f:f + 1], axis=0)).then_inc(s_gather, 16)

            pool.wait_ge(s_ids, 16)
            for f in range(F):
                gather(f)

            def body(b):
                todo, start, apart = GATHERS.get(b.q, (0, 0, 1)) if not b.last_tile else (0, 0, 1)
                f = sum(GATHERS[x][0] for x in GATHERS if x < b.q)
                order = [x for x in b.seq if is_split(x)]
                for s, tile in enumerate(order):
                    if todo and s >= start and (s - start) % apart == 0:
                        if f == 0:
                            pool.wait_ge(s_prep, b.tiles(4, 4))
                            pool.wait_ge(s_ids, b.tiles(16, 32))
                            pool.sem_inc(s_met_pool, 1)
                        gather(f)
                        f, todo = f + 1, todo - 1
                    if not on_pool(tile, b.q):
                        continue
                    n = rows_of(tile)
                    pool.wait_ge(s_hi, b.n(NS, s + 1))
                    nc.gpsimd.tensor_tensor(z_lo[0:n, s % SR], z[0:n, b.seq.index(tile) % ZR],
                                            z_hi[0:n, s % SR].bitcast(F32), ALU.subtract)\
                        .then_inc(s_lo_p, 1)
                assert todo == 0

            run_blocks(pool, body)

        @block.scalar
        def _(act):
            def copy(dst, src, **kw):
                return nc.scalar.activation(dst, src, ACT.Copy, **kw)

            def move_x(t_count, r):
                act.wait_ge(s_prep, t_count + r + 1)
                copy(x_t[:, :, 4 * r:4 * r + 4].rearrange("f b d -> f d b"),
                     t_ps[0:F, r % 2, :].rearrange("f (d b) -> f d b", d=4)).then_inc(s_xt, 1)

            def move_m0_hi(b_count, after, sums_done):
                act.wait_ge(s_pe, after)
                act.wait_ge(s_z0, sums_done)
                if b_count is not None:
                    act.wait_ge(s_mrep, b_count)
                copy(m0_hi[:], m0_ps[:]).then_inc(s_m0_hi, 1)

            def layer2_diag(q, c):
                copy(x_diag[:, :, 0:F, c], x_cols[:, CH * q:CH * (q + 1), :],
                     scale=mask[:, c:c + 1]).then_inc(s_diag, 1)

            def move_g(q, c, count):
                bank = g_bank(c)
                act.wait_ge(s_g, count)
                at = BR * q + CR * c
                copy(g2[:, :, at:at + CR], bank[:, 0:F * CR].rearrange("p (f r) -> p f r", r=CR))\
                    .then_inc(s_g2, 1)
                copy(sums[:, 1, at:at + CR], bank[:, F * CR:(F + 1) * CR]).then_inc(s_g2, 1)

            def tower_step(step, t_done):
                if step == "z2":
                    act.wait_ge(s_z2, t_done)
                    copy(sums[:, 2], t_ps[:, 1, 0:P]).then_inc(s_z2_in, 1)
                elif step == "h1":
                    act.wait_ge(s_h1_ps, t_done)
                    for m in range(H1T):
                        nc.scalar.activation(h1[:, m], t_ps[:, 1, P * m:P * (m + 1)], ACT.Relu,
                                             bias=bt1[:, m:m + 1]).then_inc(s_h1, 1)
                elif step == "h2":
                    act.wait_ge(s_h2_ps, t_done)
                    for m in range(H2T):
                        nc.scalar.activation(h2[:, m], t_ps[:, 1, P * m:P * (m + 1)], ACT.Relu,
                                             bias=bt2[:, m:m + 1]).then_inc(s_h2, 1)
                else:
                    act.wait_ge(s_y_ps, t_done)
                    copy(y[:], t_ps[0:1, 1, 0:P]).then_inc(s_y, 1)

            act.wait_ge(s_w1_in, 32)
            act.wait_ge(s_pad, 1)
            at = 0
            for lo, hi in runs(SPLIT):
                last = copy(w1_hi[:, at:at + hi - lo], w1_stage[:, lo:hi])
                at += hi - lo
            for s, i in enumerate(WHOLE):
                last = copy(w1_whole[0:rows_of((1, i)), s], w1_stage[0:rows_of((1, i)), i])
            act.wait_ge(s_const, ALL_CONSTS)
            last = copy(rep_r[:], rep)
            last.then_inc(s_w1_hi, 1)
            for r in range(4):
                move_x(0, r)
            move_m0_hi(None, L0, 1)

            def body(b):
                splits = [x for x in b.seq if is_split(x)]
                for tile in b.seq:
                    layer, i = tile
                    if layer == 1:
                        if i == ACT_M1 and b.has_prev:
                            act.wait_ge(s_pe, b.done(-1))
                            if b.has_prev2:
                                act.wait_ge(s_m1_tr, b.n(1, -1))
                            copy(m1[:], m1_ps[:, (b.q - 1) % 2]).then_inc(s_m1, 1)
                        if i == ACT_M1T and b.has_prev:
                            act.wait_ge(s_m1_tr, b.n(1))
                            if b.has_prev2:
                                act.wait_ge(s_g, b.n(CH, -CH))
                            copy(m1_t[:], t_ps[:, 0, :].rearrange("p (c m) -> p c m", m=M))\
                                .then_inc(s_m1_t, 1)
                        if 0 <= i - ACT_DIAG < CR and b.has_prev:
                            if i == ACT_DIAG:
                                act.wait_ge(s_xcols, b.tiles(2, 0 if b.q == 0 else 2))
                            layer2_diag((b.q - 1) % QB, i - ACT_DIAG)
                        if i == ACT_M0 and b.has_next:
                            move_m0_hi(b.n(GI, GI), b.done(position((0, L0 - 1))), b.n(1, 2))
                        if i in ACT_G and b.has_prev:
                            c = ACT_G.index(i)
                            move_g((b.q - 1) % QB, c, b.n(CH, c + 1 - CH))
                        if b.q == 0 and i in ACT_XD:
                            h = ACT_XD.index(i)
                            act.wait_ge(s_xd, b.tiles(2, h + 1))
                            if not b.first_tile:
                                act.wait_ge(s_diag, b.n(CR))
                            copy(x_cols[:, 8 * h:8 * h + 8],
                                 t_ps[:, 1, 0:8 * F].rearrange("p (c f) -> p c f", f=F))\
                                .then_inc(s_xcols, 1)
                        if not b.first_tile:
                            for q, at, step in ((1, ACT_Z2, "z2"), (1, ACT_H1, "h1"),
                                                (1, ACT_H2, "h2"), (2, ACT_Y, "y")):
                                if (b.q, i) == (q, at):
                                    tower_step(step, b.tiles(1))
                        if b.q == 2 and not b.last_tile and i in ACT_PREP:
                            r = ACT_PREP.index(i)
                            if r == 0:
                                act.wait_ge(s_xdram, b.tiles(32, 32))
                                act.wait_ge(s_xd, b.tiles(2, 2))
                            move_x(b.tiles(4, 4), r)
                        if b.q == QB - 1 and i == ACT_Z0:
                            act.wait_ge(s_z0, b.n(1, 1))
                            if not b.first_tile:
                                act.wait_ge(s_h1_ps, b.tiles(1))
                            copy(sums[:, 0], z0_tile[:]).then_inc(s_z0_tile, 1)
                    if is_split(tile):
                        s, n = splits.index(tile), rows_of(tile)
                        act.wait_ge(s_z, b.done(b.seq.index(tile)))
                        if (free := split_slot_free(b, splits, s)) is not None:
                            act.wait_ge(s_pe, free)
                        copy(z_hi[0:n, s % SR], z[0:n, b.seq.index(tile) % ZR]).then_inc(s_hi, 1)

            run_blocks(act, body)

            e = Place(TILES, 0)
            act.wait_ge(s_pe, e.done(-1) - L0)
            act.wait_ge(s_m1_tr, e.n(1, -1))
            copy(m1[:], m1_ps[:, (QB - 1) % 2]).then_inc(s_m1, 1)
            act.wait_ge(s_g, e.n(CH, -CH))
            for c in range(CR):
                layer2_diag(QB - 1, c)
            act.wait_ge(s_m1_tr, e.n(1))
            copy(m1_t[:], t_ps[:, 0, :].rearrange("p (c m) -> p c m", m=M)).then_inc(s_m1_t, 1)
            for c in range(CH):
                move_g(QB - 1, c, e.n(CH, c + 1 - CH))
            for step in ("z2", "h1", "h2", "y"):
                tower_step(step, TILES)

        @block.vector
        def _(dve):
            def zero_layer_products(slot, k):
                n = rows_of((0, k))
                return nc.vector.tensor_tensor(z[0:n, slot], x_rot[0:n, k], x_rot[0:n, L0], ALU.mult)

            def layer0_sums(q):
                nc.vector.tensor_reduce(z0_tile[:, BR * q:BR * (q + 1)],
                                        m0_ps[:].rearrange("p (b d) -> p b d", d=D), AX.X, ALU.add)\
                    .then_inc(s_z0, 1)

            def split_m0(blocks):
                dve.wait_ge(s_m0_hi, blocks)
                nc.vector.tensor_tensor(m0_lo[:], m0_ps[:], m0_hi[:].bitcast(F32), ALU.subtract)\
                    .then_inc(s_m0_lo, 1)

            nc.vector.memset(w1_by_maps[tail:P, :, FI - 1], 0.0).then_inc(s_pad, 1)
            dve.wait_ge(s_const, ALL_CONSTS)
            nc.vector.tensor_tensor(w0[0:SH * F, 0:L0 - 1], w0[0:SH * F, 0:L0 - 1],
                                    w0_stage[0:SH * F, 0:L0 - 1], ALU.add)
            nc.vector.tensor_tensor(w0[0:F, L0 - 1], w0[0:F, L0 - 1], w0_stage[0:F, L0 - 1], ALU.add)
            for c in range(CH):
                last = nc.vector.tensor_copy(x_diag[:, c, F], mask[:])
            last.then_inc(s_w, 1)
            dve.wait_ge(s_w1_hi, 1)
            at = 0
            for lo, hi in runs(SPLIT):
                n = hi - lo
                last = nc.vector.tensor_tensor(w1_lo[:, at:at + n], w1_stage[:, lo:hi],
                                               w1_hi[:, at:at + n].bitcast(F32), ALU.subtract)
                at += n
            last.then_inc(s_w, 1)

            dve.wait_ge(s_xrot, 16 * X_DMAS)
            for k in range(L0):
                if k >= ZR:
                    dve.wait_ge(s_pe, k - ZR + 1)
                zero_layer_products(k % ZR, k).then_inc(s_z, 1)
            dve.wait_ge(s_pe, L0)
            layer0_sums(0)
            split_m0(1)

            def split_z(b, seq, p, shift):
                tile = seq[p]
                if not is_split(tile) or on_pool(tile, (b.q - shift) % QB):
                    return
                s, n = [x for x in seq if is_split(x)].index(tile), rows_of(tile)
                dve.wait_ge(s_hi, b.n(NS, s + 1 - NS * shift))
                nc.vector.tensor_tensor(z_lo[0:n, s % SR], z[0:n, p % ZR],
                                        z_hi[0:n, s % SR].bitcast(F32), ALU.subtract)\
                    .then_inc(s_lo_v, 1)

            def body(b):
                for p, tile in enumerate(b.seq):
                    layer, i = tile
                    if layer == 1:
                        if i % FI == 0:
                            dve.wait_ge(s_mrep, b.n(GI, i // FI + 1))
                        if i < FI and i % XG == 0:
                            dve.wait_ge(s_xrep[i // XG], b.n(16 * FR, 16 * FR))
                        if i == DVE_Z0 and b.has_next:
                            dve.wait_ge(s_pe, b.done(position((0, L0 - 1))))
                            if b.q == QB - 1:
                                dve.wait_ge(s_z0_tile, b.tiles(1, 1))
                            layer0_sums((b.q + 1) % QB)
                        if i == DVE_M0 and b.has_next:
                            split_m0(b.n(1, 2))
                    elif i == 0:
                        dve.wait_ge(s_xrot, b.n(16 * X_DMAS, 32 * X_DMAS))
                    wait_slot_free(dve, b, slot_before(b, p, ZR))
                    if layer == 0:
                        zero_layer_products(p % ZR, i).then_inc(s_z, 1)
                    else:
                        n, gi, fi = rows_of(tile), i // FI, i % FI
                        nc.vector.tensor_tensor(z[0:n, p % ZR], mrep_ps[0:n, gi % 2],
                                                x_rep[0:n, fi], ALU.mult).then_inc(s_z, 1)
                    if p >= LAG:
                        split_z(b, b.seq, p - LAG, 0)
                    elif b.has_prev:
                        split_z(b, SEQ, PER + p - LAG, 1)

            def wait_slot_free(eng, b, before):
                seq, shift, p = (b.seq, 0, before) if before >= 0 else (SEQ, 1, before + PER)
                if before < 0 and not b.has_prev:
                    eng.wait_ge(s_pe, before + L0 + 1)
                    return
                tile = seq[p]
                if not is_split(tile):
                    eng.wait_ge(s_pe, b.done(before))
                else:
                    q = (b.q - shift) % QB
                    s = SPLIT.index(tile[1])
                    eng.wait_ge(s_lo_p if on_pool(tile, q) else s_lo_v, b.made_lo(q, s))

            run_blocks(dve, body)
            e = Place(TILES, 0)
            for p in range(len(SEQ_LAST) - LAG, len(SEQ_LAST)):
                split_z(e, SEQ_LAST, p, 1)

        @block.tensor
        def _(pe):
            def prep(r):
                for d in range(4):
                    last = nc.tensor.transpose(
                        t_ps[0:F, r % 2, P * d:P * (d + 1)],
                        emb[:].rearrange("p (f d) -> p f d", d=D)[:, :, 4 * r + d], ident[:])
                last.then_inc(s_prep, 1)

            def layer0(slot, k, count):
                n = rows_of((0, k))
                pe.wait_ge(s_z, count)
                nc.tensor.matmul(m0_ps[:], w0[0:n, k], z[0:n, slot], start=(k == 0), stop=(k == L0 - 1))\
                    .then_inc(s_pe, 1)

            def repeat_maps(gi, blocks, free):
                pe.wait_ge(s_m0_hi, blocks)
                pe.wait_ge(s_m0_lo, blocks)
                if free is not None:
                    pe.wait_ge(s_z, free)
                rows = slice(GR * gi, GR * (gi + 1))
                nc.tensor.matmul(mrep_ps[:, gi % 2], rep_r[rows], m0_hi[rows], start=True, stop=False)
                nc.tensor.matmul(mrep_ps[:, gi % 2], rep_r[rows], m0_lo[rows], start=False, stop=True)\
                    .then_inc(s_mrep, 1)

            def turn_m1(blocks):
                pe.wait_ge(s_m1, blocks)
                for c in range(CH):
                    last = nc.tensor.transpose(t_ps[:, 0, M * c:M * (c + 1)],
                                               m1[:, P * c:P * (c + 1)], ident[:])
                last.then_inc(s_m1_tr, 1)

            def g_chunk(c, chunks, blocks, diags):
                pe.wait_ge(s_m1_t, blocks)
                pe.wait_ge(s_diag, diags)
                if c == 0:
                    pe.wait_ge(s_w, 1)
                if chunks is not None:
                    pe.wait_ge(s_g2, chunks)
                nc.tensor.matmul(g_bank(c)[:, 0:(F + 1) * CR], m1_t[:, c],
                                 x_diag[:, c].rearrange("p f r -> p (f r)"), start=True, stop=True)\
                    .then_inc(s_g, 1)

            def layer2(part, parts, blocks):
                if part == 0:
                    pe.wait_ge(s_g2, blocks)
                per = (F + parts - 1) // parts
                for f in range(per * part, min(F, per * (part + 1))):
                    last = nc.tensor.matmul(t_ps[:, 1, 0:P], w2[:, f], g2[:, f],
                                            start=(f == 0), stop=(f == F - 1))
                if part == parts - 1:
                    last.then_inc(s_z2, 1)

            def hidden1(m, t_done):
                if m == 0:
                    pe.wait_ge(s_z2_in, t_done)
                    pe.wait_ge(s_z0_tile, t_done)
                    pe.wait_ge(s_ctx, t_done * 16)
                cols = slice(P * m, P * (m + 1))
                for k in range(3):
                    nc.tensor.matmul(t_ps[:, 1, cols], wt1[:, k, cols], sums[:, k],
                                     start=(k == 0), stop=False)
                last = nc.tensor.matmul(t_ps[:, 1, cols], wt1_ctx[:, cols], ctx_t,
                                        start=False, stop=True)
                if m == H1T - 1:
                    last.then_inc(s_h1_ps, 1)

            def hidden2(m, t_done):
                if m == 0:
                    pe.wait_ge(s_h1, t_done * H1T)
                cols = slice(P * m, P * (m + 1))
                for k in range(H1T):
                    last = nc.tensor.matmul(t_ps[:, 1, cols], wt2[:, k, cols], h1[:, k],
                                            start=(k == 0), stop=(k == H1T - 1))
                if m == H2T - 1:
                    last.then_inc(s_h2_ps, 1)

            def output(t_done):
                pe.wait_ge(s_h2, t_done * H2T)
                for k in range(H2T):
                    last = nc.tensor.matmul(t_ps[0:1, 1, 0:P], wt3[:, k:k + 1], h2[:, k],
                                            start=(k == 0), stop=(k == H2T - 1))
                last.then_inc(s_y_ps, 1)

            pe.wait_ge(s_const, ALL_CONSTS)
            pe.wait_ge(s_gather, 16 * F)
            for r in range(4):
                if r >= 2:
                    pe.wait_ge(s_xt, r - 1)
                prep(r)
            pe.wait_ge(s_w, 1)
            for k in range(L0):
                layer0(k % ZR, k, k + 1)
            pe.wait_ge(s_w1_hi, 1)
            repeat_maps(0, 1, None)
            pe.wait_ge(s_w, 2)

            def body(b):
                splits = [x for x in b.seq if is_split(x)]
                for p, tile in enumerate(b.seq):
                    layer, i = tile
                    if layer == 0:
                        if i == 0:
                            pe.wait_ge(s_m0_lo, b.n(1, 1))
                            pe.wait_ge(s_z0, b.n(1, 1))
                        layer0(p % ZR, i, b.done(p))
                        continue
                    if i == PE_MAP0:
                        repeat_maps(1, b.n(1, 1),
                                    b.done(position((1, L1 - 1)) - PER) if b.has_prev else None)
                    for gi in (2, 3):
                        if i == FI * (gi - 1) + 1:
                            repeat_maps(gi, b.n(1, 1), b.done(b.seq.index((1, FI * (gi - 1) - 1))))
                    if i == FI * 3 + 1 and b.has_next:
                        repeat_maps(0, b.n(1, 2), b.done(b.seq.index((1, FI * 3 - 1))))
                    if i == PE_M1 and b.has_prev:
                        if b.has_prev2:
                            pe.wait_ge(s_g2, b.n(2 * CH, -2 * CH))
                        turn_m1(b.n(1))
                    if i in PE_G and b.has_prev:
                        c = PE_G.index(i)
                        chunks = b.n(2 * CH, 2 * (c - 1) - 2 * CH) if b.has_prev2 or c >= 2 else None
                        if c == 1 and b.q == 2 and not b.last_tile:
                            pe.wait_ge(s_xt, b.tiles(4, 4 + 3))
                        g_chunk(c, chunks, b.n(1), b.n(CR))
                    if b.q == 0 and i in PE_XD:
                        h = PE_XD.index(i)
                        pe.wait_ge(s_xt, b.tiles(4, 4))
                        if h == 1:
                            pe.wait_ge(s_xcols, b.tiles(2, 1))
                        pe.sem_inc(s_met_pe, 1)
                        for c in range(8):
                            rows = slice(CR * (8 * h + c), CR * (8 * h + c + 1))
                            last = nc.tensor.transpose(t_ps[:, 1, F * c:F * (c + 1)],
                                                       x_t[:, rows].rearrange("f b d -> f (b d)"),
                                                       ident[0:F, 0:F])
                        last.then_inc(s_xd, 1)
                    if b.q == 1 and not b.first_tile:
                        if i in PE_Z2:
                            if i == PE_Z2[0]:
                                pe.wait_ge(s_xcols, b.tiles(2, 2))
                            layer2(PE_Z2.index(i), len(PE_Z2), b.tiles(2 * CH * QB))
                        if i in PE_H1:
                            hidden1(PE_H1.index(i), b.t)
                        if i in PE_H2:
                            hidden2(PE_H2.index(i), b.t)
                        if i == PE_Y:
                            output(b.t)
                    if b.q == 2 and not b.last_tile and i in PE_PREP:
                        r = PE_PREP.index(i)
                        if r == 0:
                            pe.wait_ge(s_gather, b.tiles(16 * F, 32 * F))
                            pe.wait_ge(s_m1_t, b.n(1))
                            if not b.first_tile:
                                pe.wait_ge(s_y, b.tiles(1))
                            else:
                                pe.wait_ge(s_xcols, 2)
                        if r >= 2:
                            pe.wait_ge(s_xt, b.tiles(4, 4 + r - 1))
                        if r != 1:
                            pe.sem_inc(s_met_pe, 1)
                        prep(r)
                    bank = m1_ps[:, b.q % 2]
                    first, last_tile = i == 0, i == L1 - 1
                    if first and b.has_prev2:
                        pe.wait_ge(s_m1, b.n(1, -1))
                    n = rows_of(tile)
                    if is_split(tile):
                        s = splits.index(tile)
                        ws = SPLIT.index(i)
                        pe.wait_ge(s_hi, b.n(NS, s + 1))
                        nc.tensor.matmul(bank, w1_hi[0:n, ws], z_hi[0:n, s % SR], start=first, stop=False)
                        nc.tensor.matmul(bank, w1_lo[0:n, ws], z_hi[0:n, s % SR], start=False, stop=False)
                        pe.wait_ge(s_lo_p if on_pool(tile, b.q) else s_lo_v, b.made_lo(b.q, s))
                        nc.tensor.matmul(bank, w1_hi[0:n, ws], z_lo[0:n, s % SR], start=False,
                                         stop=last_tile).then_inc(s_pe, 1)
                    else:
                        pe.wait_ge(s_z, b.done(p))
                        nc.tensor.matmul(bank, w1_whole[0:n, WHOLE.index(i)], z[0:n, p % ZR],
                                         start=first, stop=last_tile).then_inc(s_pe, 1)

            run_blocks(pe, body)

            e = Place(TILES, 0)
            pe.wait_ge(s_g2, e.n(2 * CH, -2 * CH))
            turn_m1(e.n(1))
            for c in range(CH):
                g_chunk(c, e.n(2 * CH, 2 * (c - 1) - 2 * CH), e.n(1), e.n(CR))
            pe.wait_ge(s_y, TILES - 1)
            layer2(0, 1, 2 * CH * QB * TILES)
            for m in range(H1T):
                hidden1(m, TILES)
            for m in range(H2T):
                hidden2(m, TILES)
            output(TILES)


def runs(tiles):
    out = []
    for i in tiles:
        if out and out[-1][1] == i:
            out[-1][1] = i + 1
        else:
            out.append([i, i + 1])
    return out


def split_slot_free(b, splits, s):
    if s >= SR:
        return b.done(b.seq.index(splits[s - SR]))
    if not b.has_prev:
        return None
    before = [x for x in SEQ if is_split(x)]
    old = max(x for x in range(NS) if x % SR == s % SR)
    return b.done(SEQ.index(before[old]) - PER)


def kernel(**inputs):
    import numpy as np
    import concourse.bacc as bacc
    from concourse.bass_utils import run_bass_kernel_spmd

    x = {k: np.asarray(v) for k, v in inputs.items()}
    f0 = x["L0_rec_f0"].reshape(F, F, M)
    f1 = x["L0_rec_f1"].reshape(F, GI, GR, M)
    field = np.arange(F)
    shift = 1 + np.arange(SH)[:, None] + SH * np.arange(L0 - 1)[None, :]
    first = np.broadcast_to(field[None, :, None], (SH, F, L0 - 1))
    second = (field[None, :, None] + shift[:, None, :]) % F
    last = (field + (F - 1) // 2) % F
    whole = FR * (FI - 1)
    p = np.arange(P)
    arrays = {
        "ids": x["ids"].reshape(TILES, P, F),
        "ctx": x["dense_ctx"].reshape(TILES, P, D).transpose(0, 2, 1),
        "w0_a": f0[first, second].reshape(SH * F, L0 - 1, M),
        "w0_b": f0[second, first].reshape(SH * F, L0 - 1, M),
        "w0_last_a": f0[field, last], "w0_last_b": f0[last, field], "w0_diag": f0[field, field],
        "w1_main": f1[:whole].reshape(FI - 1, FR, GI, GR, M).transpose(1, 3, 2, 0, 4)
        .reshape(P, GI, FI - 1, M),
        "w1_tail": f1[whole:].transpose(0, 2, 1, 3).reshape((F - whole) * GR, GI, M),
        "w2": x["L0_rec_f2"].reshape(F, M, M).transpose(1, 0, 2),
        "wt1": x["W_top1"][:3 * M].reshape(3, M, HID1).transpose(1, 0, 2),
        "wt1_ctx": x["W_top1"][3 * M:],
        "wt2": x["W_top2"].reshape(H1T, P, HID2).transpose(1, 0, 2),
        "wt3": x["W_top3"].reshape(H2T, P).T,
        "bt1": x["b_top1"].reshape(H1T, P).T,
        "bt2": x["b_top2"].reshape(H2T, P).T,
        "ident": np.eye(P, dtype=np.float32),
        "rep": (p[:, None] % GR == p[None, :] % GR).astype(np.float32),
        "mask": (p[:, None] // D == np.arange(CR)[None, :]).astype(np.float32),
        **{f"tbl_{f}": x[f"tbl_{f}"] for f in range(F)},
    }
    arrays = {k: np.ascontiguousarray(v) for k, v in arrays.items()}
    nc = bacc.Bacc("TRN2", target_bir_lowering=False, num_devices=1)
    args = {k: nc.dram_tensor(f"in_{k}", v.shape, mybir.dt.from_np(v.dtype), kind="ExternalInput").ap()
            for k, v in arrays.items()}
    out = nc.dram_tensor("out", (ROWS, 1), F32, kind="ExternalOutput").ap()
    cin_tower(nc, args, out.rearrange("(t r) o -> t (r o)", t=TILES))
    r = run_bass_kernel_spmd(nc, [{f"in_{k}": v for k, v in arrays.items()}], core_ids=[0])
    return r.results[0]["out"]
```

```python
from contextlib import ExitStack

import concourse.bass as bass
from concourse import mybir

ALU = mybir.AluOpType
ACT = mybir.ActivationFunctionType
AX = mybir.AxisListType
F32 = mybir.dt.float32
F32R = mybir.dt.float32r
I32 = mybir.dt.int32

P = 128
F = 39
D = 16
M = 128
ROWS = 1024
TILES = ROWS // P
QB = 4
BR = P // QB
NB = BR * D
SH = 3
L0 = 7
XROWS = F + (F - 1) // 2
FU = 4
GROUPS = (F + FU - 1) // FU
CH = 4
CR = P // D
HID1, HID2 = 512, 256
H1T, H2T = HID1 // P, HID2 // P

UNITS = GROUPS * CH
POOL_GROUPS = (5, 4, 6, 8)
UR = 5
PR = 7
X_DMAS = 6
L0_AFTER = {5 + 2 * k: k for k in range(L0)}
GATHERS = {0: (14, 12, 2), 1: (21, 12, 1), 2: (4, 0, 1)}

DVE_ROT = {2 * k: k for k in range(L0)}
PE_G = (24, 27, 31, 35)
PE_PREP = (14, 16, 18, 20)
PE_XD = ((3, 4), (0, 30))
PE_Z2, PE_H1, PE_H2, PE_Y = tuple(range(1, 14)), (17, 18, 19, 20), (30, 33), 39
ACT_Z0, ACT_DIAG, ACT_M0, ACT_G = 1, 12, 21, (27, 30, 34, 38)
ACT_PREP, ACT_XD, ACT_Z2, ACT_H1, ACT_H2 = (16, 18, 20, 22), ((3, 7), (0, 33)), 16, 24, 36
ACT_Y = 3
JOIN = 8
DVE_Z0, DVE_M0 = 20, 22


def group_fields(g):
    return min(FU, F - FU * g)


def for_pool(u, q):
    g, c = divmod(u, CH)
    n = POOL_GROUPS[q]
    return c == 0 or (c == 1 and g * n % GROUPS < n)


POOL_UNITS = [[u for u in range(UNITS) if for_pool(u, q)] for q in range(QB)]
DVE_UNITS = [[u for u in range(UNITS) if not for_pool(u, q)] for q in range(QB)]
ADDS = [[u for u in units if any(v % CH == u % CH for v in units if v < u)] for units in POOL_UNITS]
NP = [len(units) for units in POOL_UNITS]
PA = [len(adds) for adds in ADDS]
NV = [sum(group_fields(u // CH) for u in units) for units in DVE_UNITS]


def rows_of(k):
    return SH * F if k < L0 - 1 else 2 * F


class Place:

    def __init__(self, t, q):
        self.t, self.q = t, q
        fixed = isinstance(t, int)
        self.first_tile = fixed and t == 0
        self.last_tile = fixed and t == TILES - 1
        self.has_prev = not (self.first_tile and q == 0)
        self.has_prev2 = not (self.first_tile and q < 2)
        self.has_next = not (self.last_tile and q == QB - 1)
        self.has_next2 = not (self.last_tile and q >= QB - 2)

    def n(self, per, plus=0):
        return self.t * (QB * per) + (self.q * per + plus)

    def sum(self, per, plus=0, back=0):
        q = self.q - back
        before = sum(per[:q % QB]) - (0 if q >= 0 else sum(per))
        return self.t * sum(per) + (before + plus)

    def tiles(self, per, plus=0):
        return self.t * per + plus


def run_blocks(eng, body):
    for q in range(QB):
        body(Place(0, q))
    with eng.Fori(1, TILES - 1) as t:
        for q in range(QB):
            body(Place(t, q))
    for q in range(QB):
        body(Place(TILES - 1, q))


def bank_read(eng, b, u, s_acc_v, s_prod):
    back = 0 if u >= 0 else 1
    u, q = u % UNITS, (b.q - back) % QB
    if for_pool(u, q):
        eng.wait_ge(s_prod, b.sum(NP, POOL_UNITS[q].index(u) + 1, back))
    else:
        eng.wait_ge(s_acc_v, b.sum(NV, added(u, q), back))


def added(u, q):
    return sum(group_fields(x // CH) for x in DVE_UNITS[q] if x <= u)


def additions(j, q):
    u = POOL_UNITS[q][j]
    if u not in ADDS[q]:
        u = min(v for v in ADDS[q] if v % CH == u % CH)
    return ADDS[q].index(u) + 1


def prod_slot(q, j):
    assert sum(NP) % PR == 0
    return (sum(NP[:q]) + j) % PR


def cin_tower(nc, a, out):
    with ExitStack() as ctx:
        def sb(name, shape, dt=F32):
            return ctx.enter_context(nc.sbuf_tensor(name, shape, dt))

        def ps(name, shape):
            return ctx.enter_context(nc.psum_tensor(name, shape, F32))

        def sem(name):
            return ctx.enter_context(nc.semaphore(name))

        w0 = sb("w0", [P, L0, M])
        w1_hi = sb("w1_hi", [P, F, M], F32R)
        w1_lo = sb("w1_lo", [P, F, M], F32R)
        w2 = sb("w2", [P, F, M])
        wt1 = sb("wt1", [P, 3, HID1])
        wt2 = sb("wt2", [P, H1T, HID2])
        wt3 = sb("wt3", [P, H2T])
        bt1 = sb("bt1", [P, H1T])
        bt2 = sb("bt2", [P, H2T])
        ident = sb("ident", [P, P])
        mask = sb("mask", [P, CR])
        ids = sb("ids", [P, F], I32)
        emb = sb("emb", [P, F * D])
        x_t_store = sb("x_t_store", [P, P * D])
        x_t = x_t_store[0:F].rearrange("f (b d) -> f b d", d=D)
        wt1_ctx = x_t_store[64:64 + D, 0:HID1]
        ctx_t = x_t_store[64:64 + D, HID1:HID1 + P]
        x_cols = sb("x_cols", [P, P // CR, F])
        x_rot = sb("x_rot", [P, L0 + 1, NB])
        z = sb("z", [P, L0, NB])
        m0_hi = sb("m0_hi", [P, 2, NB], F32R)
        m0_lo = sb("m0_lo", [P, 2, NB], F32R)
        m1_t = sb("m1_t", [P, 2, CH, M])
        prod = sb("prod", [P, PR, FU, M])
        acc_p = sb("acc_p", [P, 2, FU, M])
        half = sb("half", [P, 2, M])
        part = sb("part", [P, M])
        acc_v = sb("acc_v", [P, 2, CH - 1, M])
        x_diag = sb("x_diag", [P, CH, F + 1, CR])
        g2 = sb("g2", [P, F, P])
        z0_tile = sb("z0_tile", [P, P])
        sums = sb("sums", [P, 3, P])
        h1 = sb("h1", [P, H1T, P])
        h2 = sb("h2", [P, H2T, P])
        y = sb("y", [1, P])
        w1_in = g2[:]
        w0_stage = prod[:, 0:2].rearrange("p a f m -> p (a f) m")

        u_ps = ps("u_ps", [P, UR, FU * M])
        m0_ps = ps("m0_ps", [P, NB])
        g_ps = ps("g_ps", [P, 512])
        t_ps = ps("t_ps", [P, 512])

        def g_bank(c):
            return g_ps if c % 2 == 0 else m0_ps

        def prep_bank(r):
            return g_ps if r % 2 == 0 else t_ps

        x_dram = nc.dram_tensor("x_scratch", (TILES, XROWS, P * D), F32, kind="Internal").ap()

        s_const = sem("s_const")
        s_w1_in = sem("s_w1_in")
        s_w1_hi = sem("s_w1_hi")
        s_w = sem("s_w")
        s_ids = sem("s_ids")
        s_gather = sem("s_gather")
        s_prep = sem("s_prep")
        s_xt = sem("s_xt")
        s_xdram = sem("s_xdram")
        s_xrot = sem("s_xrot")
        s_xd = sem("s_xd")
        s_xcols = sem("s_xcols")
        s_z = sem("s_z")
        s_l0 = sem("s_l0")
        s_m0_hi = sem("s_m0_hi")
        s_m0_lo = sem("s_m0_lo")
        s_z0 = sem("s_z0")
        s_z0_tile = sem("s_z0_tile")
        s_u = sem("s_u")
        s_acc_v = sem("s_acc_v")
        s_m1 = sem("s_m1")
        s_prod = sem("s_prod")
        s_acc_p = sem("s_acc_p")
        s_half = sem("s_half")
        s_joined = sem("s_joined")
        s_fold = sem("s_fold")
        s_diag = sem("s_diag")
        s_g = sem("s_g")
        s_g2 = sem("s_g2")
        s_z2 = sem("s_z2")
        s_z2_in = sem("s_z2_in")
        s_ctx = sem("s_ctx")
        s_h1_ps = sem("s_h1_ps")
        s_h1 = sem("s_h1")
        s_h2_ps = sem("s_h2_ps")
        s_h2 = sem("s_h2")
        s_y_ps = sem("s_y_ps")
        s_y = sem("s_y")
        s_out = sem("s_out")

        s_met_pe, s_met_pool, s_met_sp = sem("s_met_pe"), sem("s_met_pool"), sem("s_met_sp")

        CONSTS = [
            (w0[0:SH * F, 0:L0 - 1, :], a["w0_a"]), (w0[0:F, L0 - 1, :], a["w0_last_a"]),
            (w0[F:2 * F, L0 - 1, :], a["w0_diag"]),
            (w0_stage[0:SH * F, 0:L0 - 1, :], a["w0_b"]), (w0_stage[0:F, L0 - 1, :], a["w0_last_b"]),
            (ident[:], a["ident"]), (mask[:], a["mask"]),
            (w2[:], a["w2"]),
            (wt1[:], a["wt1"]), (wt1_ctx, a["wt1_ctx"]), (wt2[:], a["wt2"]), (wt3[:], a["wt3"]),
            (bt1[:], a["bt1"]), (bt2[:], a["bt2"]),
        ]
        ALL_CONSTS = 16 * len(CONSTS)

        block = ctx.enter_context(nc.Block())

        @block.sync
        def _(sp):
            def settled():
                sp.sem_inc(s_met_sp, 1)

            def load_ids(t):
                sp.dma_start(ids[:], a["ids"][bass.ds(t, 1)].rearrange("a p f -> p (a f)"))\
                    .then_inc(s_ids, 16)

            def store_x(t):
                for lo, n in ((0, F), (F, XROWS - F)):
                    sp.dma_start(x_dram[bass.ds(t, 1), lo:lo + n].rearrange("a f c -> f (a c)"),
                                 x_t[0:n].rearrange("f b d -> f (b d)")).then_inc(s_xdram, 16)

            def x_at(t, q, row, pattern):
                return bass.AP(x_dram.tensor, t * (XROWS * P * D) + (row * P * D + q * NB),
                               [*pattern, [1, NB]])

            def load_rot(t, q):
                row = P * D
                for s in range(SH):
                    n = L0 if s == 0 else L0 - 1
                    sp.dma_start(x_rot[F * s:F * (s + 1), 0:n, :],
                                 x_at(t, q, 1 + s, [[row, F], [SH * row, n]])).then_inc(s_xrot, 16)
                sp.dma_start(x_rot[F:2 * F, L0 - 1:L0 + 1, :],
                             x_at(t, q, 0, [[row, F], [0, 2]])).then_inc(s_xrot, 16)
                for s in (0, 2):
                    sp.dma_start(x_rot[F * s:F * (s + 1), L0, :],
                                 x_at(t, q, 0, [[row, F]])).then_inc(s_xrot, 16)

            load_ids(0)
            for dst, src in CONSTS:
                sp.dma_start(dst, src).then_inc(s_const, 16)
            sp.dma_start(w1_in, a["w1"]).then_inc(s_w1_in, 16)
            sp.wait_ge(s_xt, 4)
            store_x(0)
            sp.wait_ge(s_xdram, 32)
            load_rot(0, 0)
            sp.wait_ge(s_z, L0)
            load_rot(0, 1)

            def body(b):
                if b.q == 0 and not b.last_tile:
                    sp.wait_ge(s_gather, b.tiles(16 * F, 16 * F))
                    settled()
                    load_ids(b.t + 1)
                if b.q == 0 and not b.first_tile:
                    sp.dma_start(ctx_t, a["ctx"][bass.ds(b.t - 1, 1)].rearrange("a d r -> d (a r)"))\
                        .then_inc(s_ctx, 16)
                if b.q == 2 and not b.last_tile:
                    sp.wait_ge(s_xt, b.tiles(4, 8))
                    settled()
                    store_x(b.t + 1)
                    sp.wait_ge(s_xdram, b.tiles(32, 64))
                    settled()
                if b.has_next2:
                    sp.wait_ge(s_z, b.n(L0, 2 * L0))
                    settled()
                    load_rot(*((b.t, b.q + 2) if b.q < QB - 2 else (b.t + 1, b.q + 2 - QB)))
                if b.q == 2 and not b.first_tile:
                    sp.wait_ge(s_y, b.tiles(1))
                    settled()
                    sp.dma_start(out[bass.ds(b.t - 1, 1)], y[:])\
                        .then_inc(s_out, 16)
                if b.q == QB - 1 and not b.first_tile:
                    sp.wait_ge(s_out, b.tiles(16))
                    settled()

            run_blocks(sp, body)
            sp.dma_start(ctx_t, a["ctx"][TILES - 1]).then_inc(s_ctx, 16)
            sp.wait_ge(s_y, TILES)
            sp.dma_start(out[TILES - 1:TILES], y[:]).then_inc(s_out, 16)
            sp.wait_ge(s_out, 16 * TILES)

        @block.gpsimd
        def _(pool):
            def gather(f):
                nc.gpsimd.indirect_dma_start(
                    emb[:, D * f:D * (f + 1)], None, a[f"tbl_{f}"],
                    bass.IndirectOffsetOnAxis(ap=ids[:, f:f + 1], axis=0)).then_inc(s_gather, 16)

            def join_chunk1(q, blocks):
                pool.wait_ge(s_m1, blocks)
                pool.wait_ge(s_fold, 2 * blocks)
                nc.gpsimd.tensor_tensor(m1_t[:, q % 2, 1], m1_t[:, q % 2, 1], part[:], ALU.add)\
                    .then_inc(s_joined, 1)

            def fold(c, to, sums, halves, folds):
                pool.wait_ge(s_acc_p, sums)
                if folds is not None:
                    pool.wait_ge(s_fold, folds)
                nc.gpsimd.tensor_tensor(half[:], acc_p[:, c, 0:2], acc_p[:, c, 2:4], ALU.add)\
                    .then_inc(s_half, 1)
                pool.wait_ge(s_half, halves)
                nc.gpsimd.tensor_tensor(to, half[:, 0], half[:, 1], ALU.add)\
                    .then_inc(s_fold, 1)

            pool.wait_ge(s_ids, 16)
            for f in range(F):
                gather(f)

            def body(b):
                todo, start, apart = GATHERS.get(b.q, (0, 0, 1)) if not b.last_tile else (0, 0, 1)
                f = sum(GATHERS[x][0] for x in GATHERS if x < b.q)
                for u in range(UNITS):
                    if u == JOIN and b.has_prev:
                        join_chunk1(b.q + 1, b.n(1))
                    if todo and u >= start and (u - start) % apart == 0:
                        if f == 0:
                            pool.wait_ge(s_prep, b.tiles(4, 4))
                            pool.wait_ge(s_ids, b.tiles(16, 32))
                            pool.sem_inc(s_met_pool, 1)
                        gather(f)
                        f, todo = f + 1, todo - 1
                    if not for_pool(u, b.q):
                        continue
                    (g, c), j = divmod(u, CH), POOL_UNITS[b.q].index(u)
                    if u in ADDS[b.q]:
                        n, own = group_fields(g), [v for v in POOL_UNITS[b.q] if v % CH == c]
                        second = u == own[1]
                        assert not second or n == FU
                        pool.wait_ge(s_prod, b.sum(NP, j + 1))
                        if second:
                            if b.has_prev:
                                pool.wait_ge(s_half, b.n(2))
                            before = prod[:, prod_slot(b.q, POOL_UNITS[b.q].index(own[0])), 0:n]
                        else:
                            last = own[own.index(u) - 1]
                            pool.wait_ge(s_acc_p, b.sum(PA, ADDS[b.q].index(last) + 1))
                            before = acc_p[:, c, 0:n]
                        nc.gpsimd.tensor_tensor(acc_p[:, c, 0:n], before,
                                                prod[:, prod_slot(b.q, j), 0:n], ALU.add)\
                            .then_inc(s_acc_p, 1)
                if b.has_prev2:
                    pool.wait_ge(s_g, b.n(CH, -CH))
                fold(0, m1_t[:, b.q % 2, 0], b.sum(PA, PA[b.q]), b.n(2, 1), b.n(2) if b.has_prev else None)
                fold(1, part[:], b.sum(PA, PA[b.q]), b.n(2, 2), b.n(2, 1))
                assert todo == 0

            run_blocks(pool, body)
            join_chunk1(QB - 1, QB * TILES)

        @block.scalar
        def _(act):
            def copy(dst, src, **kw):
                return nc.scalar.activation(dst, src, ACT.Copy, **kw)

            def move_x(t_count, r):
                act.wait_ge(s_prep, t_count + r + 1)
                copy(x_t[:, :, 4 * r:4 * r + 4].rearrange("f b d -> f d b"),
                     prep_bank(r)[0:F].rearrange("f (d b) -> f d b", d=4)).then_inc(s_xt, 1)

            def move_m0_hi(q, tiles_done, sums_done):
                act.wait_ge(s_l0, tiles_done)
                act.wait_ge(s_z0, sums_done)
                copy(m0_hi[:, q % 2], m0_ps[:]).then_inc(s_m0_hi, 1)

            def move_cols(half, count):
                act.wait_ge(s_xd, count)
                copy(x_cols[:, 8 * half:8 * half + 8],
                     t_ps[:, 0:8 * F].rearrange("p (c f) -> p c f", f=F)).then_inc(s_xcols, 1)

            def layer2_diag(q, c):
                copy(x_diag[:, :, 0:F, c], x_cols[:, CH * q:CH * (q + 1), :],
                     scale=mask[:, c:c + 1]).then_inc(s_diag, 1)

            def move_g(q, c, count):
                bank = g_bank(c)
                act.wait_ge(s_g, count)
                at = BR * q + CR * c
                copy(g2[:, :, at:at + CR], bank[:, 0:F * CR].rearrange("p (f r) -> p f r", r=CR))\
                    .then_inc(s_g2, 1)
                copy(sums[:, 1, at:at + CR], bank[:, F * CR:(F + 1) * CR]).then_inc(s_g2, 1)

            def tower_step(step, t_done):
                if step == "z2":
                    act.wait_ge(s_z2, t_done)
                    copy(sums[:, 2], t_ps[:, 0:P]).then_inc(s_z2_in, 1)
                elif step == "h1":
                    act.wait_ge(s_h1_ps, t_done)
                    for m in range(H1T):
                        nc.scalar.activation(h1[:, m], t_ps[:, P * m:P * (m + 1)], ACT.Relu,
                                             bias=bt1[:, m:m + 1]).then_inc(s_h1, 1)
                elif step == "h2":
                    act.wait_ge(s_h2_ps, t_done)
                    for m in range(H2T):
                        nc.scalar.activation(h2[:, m], t_ps[:, P * m:P * (m + 1)], ACT.Relu,
                                             bias=bt2[:, m:m + 1]).then_inc(s_h2, 1)
                else:
                    act.wait_ge(s_y_ps, t_done)
                    copy(y[:], t_ps[0:1, 0:P]).then_inc(s_y, 1)

            act.wait_ge(s_const, ALL_CONSTS)
            act.wait_ge(s_w1_in, 16)
            copy(w1_hi[:], w1_in).then_inc(s_w1_hi, 1)
            for r in range(4):
                move_x(0, r)
            move_cols(0, 1)
            move_m0_hi(0, L0, 1)

            def body(b):
                for u in range(UNITS):
                    if 0 <= u - ACT_DIAG < CR and b.has_prev:
                        if u == ACT_DIAG:
                            act.wait_ge(s_xcols, b.tiles(2, (0, 1, 1, 2)[b.q]))
                            if b.has_prev2:
                                act.wait_ge(s_g, b.n(CH, -CH))
                        layer2_diag((b.q - 1) % QB, u - ACT_DIAG)
                    if u == ACT_M0 and b.has_next:
                        act.wait_ge(s_u, b.n(UNITS))
                        move_m0_hi(b.q + 1, b.n(L0, 2 * L0), b.n(1, 2))
                    if u in ACT_G and b.has_prev:
                        c = ACT_G.index(u)
                        move_g((b.q - 1) % QB, c, b.n(CH, c + 1 - CH))
                    if (b.q, u) == ACT_XD[1]:
                        if not b.first_tile:
                            act.wait_ge(s_diag, b.n(CR))
                            act.wait_ge(s_acc_v, b.sum(NV))
                        move_cols(1, b.tiles(2, 2))
                    if (b.q, u) == ACT_XD[0] and not b.last_tile:
                        act.wait_ge(s_diag, b.n(CR, -CR))
                        act.wait_ge(s_acc_v, b.sum(NV, 0, 1))
                        move_cols(0, b.tiles(2, 3))
                    if not b.first_tile:
                        for q, at, step in ((1, ACT_Z2, "z2"), (1, ACT_H1, "h1"),
                                            (1, ACT_H2, "h2"), (2, ACT_Y, "y")):
                            if (b.q, u) == (q, at):
                                tower_step(step, b.tiles(1))
                    if b.q == 2 and not b.last_tile and u in ACT_PREP:
                        r = ACT_PREP.index(u)
                        if r == 0:
                            act.wait_ge(s_xdram, b.tiles(32, 32))
                            act.wait_ge(s_xd, b.tiles(2, 2))
                        move_x(b.tiles(4, 4), r)
                    if b.q == QB - 1 and u == ACT_Z0:
                        act.wait_ge(s_z0, b.n(1, 1))
                        if not b.first_tile:
                            act.wait_ge(s_h1_ps, b.tiles(1))
                        copy(sums[:, 0], z0_tile[:]).then_inc(s_z0_tile, 1)
                    if for_pool(u, b.q):
                        (g, c), j = divmod(u, CH), POOL_UNITS[b.q].index(u)
                        if u == 0:
                            act.wait_ge(s_xcols, b.tiles(2, 1 if b.q < 2 else 2))
                        if j >= PR:
                            act.wait_ge(s_acc_p, b.sum(PA, additions(j - PR, b.q)))
                        elif b.has_prev:
                            old = NP[(b.q - 1) % QB] + j - PR
                            act.wait_ge(s_acc_p, b.sum(PA, additions(old, (b.q - 1) % QB), 1))
                        act.wait_ge(s_u, b.n(UNITS, u + 1))
                        for f in range(group_fields(g)):
                            last = copy(prod[:, prod_slot(b.q, j), f], u_ps[:, u % UR, M * f:M * (f + 1)],
                                        scale=x_cols[:, CH * b.q + c, FU * g + f:FU * g + f + 1])
                        last.then_inc(s_prod, 1)

            run_blocks(act, body)

            e = Place(TILES, 0)
            act.wait_ge(s_g, e.n(CH, -CH))
            for c in range(CR):
                layer2_diag(QB - 1, c)
            for c in range(CH):
                move_g(QB - 1, c, e.n(CH, c + 1 - CH))
            for step in ("z2", "h1", "h2", "y"):
                tower_step(step, TILES)

        @block.vector
        def _(dve):
            def layer0_products(k):
                n = rows_of(k)
                nc.vector.tensor_tensor(z[0:n, k], x_rot[0:n, k], x_rot[0:n, L0], ALU.mult)\
                    .then_inc(s_z, 1)

            def layer0_sums(q):
                nc.vector.tensor_reduce(z0_tile[:, BR * q:BR * (q + 1)],
                                        m0_ps[:].rearrange("p (b d) -> p b d", d=D), AX.X, ALU.add)\
                    .then_inc(s_z0, 1)

            def split_m0(q, blocks):
                dve.wait_ge(s_m0_hi, blocks)
                nc.vector.tensor_tensor(m0_lo[:, q % 2], m0_ps[:], m0_hi[:, q % 2].bitcast(F32),
                                        ALU.subtract).then_inc(s_m0_lo, 1)

            dve.wait_ge(s_const, ALL_CONSTS)
            nc.vector.tensor_tensor(w0[0:SH * F, 0:L0 - 1], w0[0:SH * F, 0:L0 - 1],
                                    w0_stage[0:SH * F, 0:L0 - 1], ALU.add)
            nc.vector.tensor_tensor(w0[0:F, L0 - 1], w0[0:F, L0 - 1], w0_stage[0:F, L0 - 1], ALU.add)
            for c in range(CH):
                last = nc.vector.tensor_copy(x_diag[:, c, F], mask[:])
            last.then_inc(s_w, 1)
            dve.wait_ge(s_w1_hi, 1)
            nc.vector.tensor_tensor(w1_lo[:], w1_in, w1_hi[:].bitcast(F32), ALU.subtract)\
                .then_inc(s_w, 1)

            dve.wait_ge(s_xrot, 16 * X_DMAS)
            for k in range(L0):
                layer0_products(k)
            dve.wait_ge(s_l0, L0)
            layer0_sums(0)
            split_m0(0, 1)

            def body(b):
                for u in range(UNITS):
                    if u in DVE_ROT and b.has_next:
                        k = DVE_ROT[u]
                        if k == 0:
                            dve.wait_ge(s_xrot, b.n(16 * X_DMAS, 32 * X_DMAS))
                        dve.wait_ge(s_l0, b.n(L0, k + 1))
                        layer0_products(k)
                    if u == DVE_Z0 and b.has_next:
                        dve.wait_ge(s_l0, b.n(L0, 2 * L0))
                        if b.q == QB - 1:
                            dve.wait_ge(s_z0_tile, b.tiles(1, 1))
                        layer0_sums((b.q + 1) % QB)
                    if u == DVE_M0 and b.has_next:
                        split_m0(b.q + 1, b.n(1, 2))
                    if for_pool(u, b.q):
                        continue
                    g, c = divmod(u, CH)
                    if u == DVE_UNITS[b.q][0]:
                        dve.wait_ge(s_xcols, b.tiles(2, 1 if b.q < 2 else 2))
                        if b.has_prev:
                            dve.wait_ge(s_m1, b.n(1))
                    dve.wait_ge(s_u, b.n(UNITS, u + 1))
                    for f in range(group_fields(g)):
                        acc = acc_v[:, f % 2, c - 1]
                        u_f = u_ps[:, u % UR, M * f:M * (f + 1)]
                        x_f = x_cols[:, CH * b.q + c, FU * g + f:FU * g + f + 1]
                        before = added(u, b.q) - group_fields(g) + f - 1
                        if b.has_prev or before > 0:
                            dve.wait_ge(s_acc_v, b.sum(NV, before))
                        if u == min(v for v in DVE_UNITS[b.q] if v % CH == c) and f < 2:
                            nc.vector.tensor_scalar(acc, u_f, x_f, None, ALU.mult).then_inc(s_acc_v, 1)
                        else:
                            nc.vector.scalar_tensor_tensor(acc, u_f, x_f, acc, ALU.mult, ALU.add)\
                                .then_inc(s_acc_v, 1)
                dve.wait_ge(s_acc_v, b.sum(NV, NV[b.q]))
                if b.has_prev2:
                    dve.wait_ge(s_g, b.n(CH, -CH))
                nc.vector.tensor_tensor(m1_t[:, b.q % 2, 1:CH], acc_v[:, 0], acc_v[:, 1], ALU.add)\
                    .then_inc(s_m1, 1)

            run_blocks(dve, body)

        @block.tensor
        def _(pe):
            def prep(r):
                for d in range(4):
                    last = nc.tensor.transpose(
                        prep_bank(r)[0:F, P * d:P * (d + 1)],
                        emb[:].rearrange("p (f d) -> p f d", d=D)[:, :, 4 * r + d], ident[:])
                last.then_inc(s_prep, 1)

            def layer0(k, count):
                n = rows_of(k)
                pe.wait_ge(s_z, count)
                nc.tensor.matmul(m0_ps[:], w0[0:n, k], z[0:n, k], start=(k == 0), stop=(k == L0 - 1))\
                    .then_inc(s_l0, 1)

            def turn_x(half):
                for c in range(8):
                    rows = slice(CR * (8 * half + c), CR * (8 * half + c + 1))
                    last = nc.tensor.transpose(t_ps[:, F * c:F * (c + 1)],
                                               x_t[:, rows].rearrange("f b d -> f (b d)"),
                                               ident[0:F, 0:F])
                last.then_inc(s_xd, 1)

            def g_chunk(c, q, blocks, diags, chunks):
                if c == 0:
                    pe.wait_ge(s_m1, blocks)
                    pe.wait_ge(s_fold, blocks * 2)
                    pe.wait_ge(s_joined, blocks)
                    pe.wait_ge(s_diag, diags)
                    pe.wait_ge(s_w, 1)
                if chunks is not None:
                    pe.wait_ge(s_g2, chunks)
                nc.tensor.matmul(g_bank(c)[:, 0:(F + 1) * CR], m1_t[:, q % 2, c],
                                 x_diag[:, c].rearrange("p f r -> p (f r)"), start=True, stop=True)\
                    .then_inc(s_g, 1)

            def layer2(part, parts, blocks):
                if part == 0:
                    pe.wait_ge(s_g2, blocks)
                per = (F + parts - 1) // parts
                for f in range(per * part, min(F, per * (part + 1))):
                    last = nc.tensor.matmul(t_ps[:, 0:P], w2[:, f], g2[:, f],
                                            start=(f == 0), stop=(f == F - 1))
                if part == parts - 1:
                    last.then_inc(s_z2, 1)

            def hidden1(m, t_done):
                if m == 0:
                    pe.wait_ge(s_z2_in, t_done)
                    pe.wait_ge(s_z0_tile, t_done)
                    pe.wait_ge(s_ctx, t_done * 16)
                cols = slice(P * m, P * (m + 1))
                for k in range(3):
                    nc.tensor.matmul(t_ps[:, cols], wt1[:, k, cols], sums[:, k],
                                     start=(k == 0), stop=False)
                last = nc.tensor.matmul(t_ps[:, cols], wt1_ctx[:, cols], ctx_t,
                                        start=False, stop=True)
                if m == H1T - 1:
                    last.then_inc(s_h1_ps, 1)

            def hidden2(m, t_done):
                if m == 0:
                    pe.wait_ge(s_h1, t_done * H1T)
                cols = slice(P * m, P * (m + 1))
                for k in range(H1T):
                    last = nc.tensor.matmul(t_ps[:, cols], wt2[:, k, cols], h1[:, k],
                                            start=(k == 0), stop=(k == H1T - 1))
                if m == H2T - 1:
                    last.then_inc(s_h2_ps, 1)

            def output(t_done):
                pe.wait_ge(s_h2, t_done * H2T)
                for k in range(H2T):
                    last = nc.tensor.matmul(t_ps[0:1, 0:P], wt3[:, k:k + 1], h2[:, k],
                                            start=(k == 0), stop=(k == H2T - 1))
                last.then_inc(s_y_ps, 1)

            pe.wait_ge(s_const, ALL_CONSTS)
            pe.wait_ge(s_gather, 16 * F)
            for r in range(4):
                if r >= 2:
                    pe.wait_ge(s_xt, r - 1)
                prep(r)
            pe.wait_ge(s_xt, 4)
            turn_x(0)
            pe.wait_ge(s_w, 1)
            for k in range(L0):
                layer0(k, k + 1)
            pe.wait_ge(s_w1_hi, 1)
            pe.wait_ge(s_w, 2)

            def body(b):
                for u in range(UNITS):
                    if u in PE_G and b.has_prev:
                        c = PE_G.index(u)
                        if c == 0 and b.q == 2 and not b.last_tile:
                            pe.wait_ge(s_xt, b.tiles(4, 4 + 3))
                        if c == 1 and b.has_next:
                            pe.wait_ge(s_m0_lo, b.n(1, 2))
                        chunks = b.n(2 * CH, 2 * (c - 1) - 2 * CH) if b.has_prev2 or c >= 2 else None
                        g_chunk(c, b.q + 1, b.n(1), b.n(CR), chunks)
                    if (b.q, u) == PE_XD[1]:
                        pe.wait_ge(s_xcols, b.tiles(2, 1))
                        pe.sem_inc(s_met_pe, 1)
                        turn_x(1)
                    if (b.q, u) == PE_XD[0] and not b.last_tile:
                        pe.wait_ge(s_xt, b.tiles(4, 8))
                        pe.sem_inc(s_met_pe, 1)
                        turn_x(0)
                    if b.q == 1 and not b.first_tile:
                        if u in PE_Z2:
                            if u == PE_Z2[0]:
                                pe.wait_ge(s_xcols, b.tiles(2, 2))
                            layer2(PE_Z2.index(u), len(PE_Z2), b.tiles(2 * CH * QB))
                        if u in PE_H1:
                            hidden1(PE_H1.index(u), b.t)
                        if u in PE_H2:
                            hidden2(PE_H2.index(u), b.t)
                        if u == PE_Y:
                            output(b.t)
                    if b.q == 2 and not b.last_tile and u in PE_PREP:
                        r = PE_PREP.index(u)
                        if r == 0:
                            pe.wait_ge(s_gather, b.tiles(16 * F, 32 * F))
                            pe.wait_ge(s_g2, b.n(2 * CH, -2 * CH))
                        if r == 1:
                            if not b.first_tile:
                                pe.wait_ge(s_y, b.tiles(1))
                            else:
                                pe.wait_ge(s_xcols, 2)
                        if r >= 2:
                            pe.wait_ge(s_xt, b.tiles(4, 4 + r - 1))
                        pe.sem_inc(s_met_pe, 1)
                        prep(r)
                    if u == 0:
                        pe.wait_ge(s_m0_hi, b.n(1, 1))
                        pe.wait_ge(s_m0_lo, b.n(1, 1))
                    g, c = divmod(u, CH)
                    if u >= UR or b.has_prev:
                        bank_read(pe, b, u - UR, s_acc_v, s_prod)
                    fields = slice(FU * g, FU * g + group_fields(g))
                    cols = slice(P * c, P * (c + 1))
                    hi, lo = m0_hi[:, b.q % 2, cols], m0_lo[:, b.q % 2, cols]
                    w_hi = w1_hi[:, fields].rearrange("p f m -> p (f m)")
                    w_lo = w1_lo[:, fields].rearrange("p f m -> p (f m)")
                    bank = u_ps[:, u % UR, 0:group_fields(g) * M]
                    nc.tensor.matmul(bank, hi, w_hi, start=True, stop=False)
                    nc.tensor.matmul(bank, hi, w_lo, start=False, stop=False)
                    nc.tensor.matmul(bank, lo, w_hi, start=False, stop=True).then_inc(s_u, 1)
                    if u in L0_AFTER and b.has_next:
                        k = L0_AFTER[u]
                        if k == 0:
                            pe.wait_ge(s_m0_lo, b.n(1, 1))
                            if b.has_prev2:
                                pe.wait_ge(s_g2, b.n(2 * CH, -2 * CH))
                        layer0(k, b.n(L0, L0 + k + 1))

            run_blocks(pe, body)

            e = Place(TILES, 0)
            for c in range(CH):
                g_chunk(c, 1, QB * TILES, e.n(CR), e.n(2 * CH, 2 * (c - 1) - 2 * CH))
            pe.wait_ge(s_y, TILES - 1)
            layer2(0, 1, 2 * CH * QB * TILES)
            for m in range(H1T):
                hidden1(m, TILES)
            for m in range(H2T):
                hidden2(m, TILES)
            output(TILES)


def kernel(**inputs):
    import numpy as np
    import concourse.bacc as bacc
    from concourse.bass_utils import run_bass_kernel_spmd

    x = {k: np.asarray(v) for k, v in inputs.items()}
    f0 = x["L0_rec_f0"].reshape(F, F, M)
    field = np.arange(F)
    shift = 1 + np.arange(SH)[:, None] + SH * np.arange(L0 - 1)[None, :]
    first = np.broadcast_to(field[None, :, None], (SH, F, L0 - 1))
    second = (field[None, :, None] + shift[:, None, :]) % F
    last = (field + (F - 1) // 2) % F
    p = np.arange(P)
    arrays = {
        "ids": x["ids"].reshape(TILES, P, F),
        "ctx": x["dense_ctx"].reshape(TILES, P, D).transpose(0, 2, 1),
        "w0_a": f0[first, second].reshape(SH * F, L0 - 1, M),
        "w0_b": f0[second, first].reshape(SH * F, L0 - 1, M),
        "w0_last_a": f0[field, last], "w0_last_b": f0[last, field], "w0_diag": f0[field, field],
        "w1": x["L0_rec_f1"].reshape(F, M, M).transpose(1, 0, 2),
        "w2": x["L0_rec_f2"].reshape(F, M, M).transpose(1, 0, 2),
        "wt1": x["W_top1"][:3 * M].reshape(3, M, HID1).transpose(1, 0, 2),
        "wt1_ctx": x["W_top1"][3 * M:],
        "wt2": x["W_top2"].reshape(H1T, P, HID2).transpose(1, 0, 2),
        "wt3": x["W_top3"].reshape(H2T, P).T,
        "bt1": x["b_top1"].reshape(H1T, P).T,
        "bt2": x["b_top2"].reshape(H2T, P).T,
        "ident": np.eye(P, dtype=np.float32),
        "mask": (p[:, None] // D == np.arange(CR)[None, :]).astype(np.float32),
        **{f"tbl_{f}": x[f"tbl_{f}"] for f in range(F)},
    }
    arrays = {k: np.ascontiguousarray(v) for k, v in arrays.items()}
    nc = bacc.Bacc("TRN2", target_bir_lowering=False, num_devices=1)
    args = {k: nc.dram_tensor(f"in_{k}", v.shape, mybir.dt.from_np(v.dtype), kind="ExternalInput").ap()
            for k, v in arrays.items()}
    out = nc.dram_tensor("out", (ROWS, 1), F32, kind="ExternalOutput").ap()
    cin_tower(nc, args, out.rearrange("(t r) o -> t (r o)", t=TILES))
    r = run_bass_kernel_spmd(nc, [{f"in_{k}": v for k, v in arrays.items()}], core_ids=[0])
    return r.results[0]["out"]
```
